# Optimizing a Trainium2 kernel written in Bass

```python
import numpy as np
import jax
import jax.numpy as jnp

def _softmax(x, axis=-1):
    return jax.nn.softmax(x, axis=axis)

def _gelu(x):
    return jax.nn.gelu(x, approximate=True)

def _silu(x):
    return jax.nn.silu(x)

def _sigmoid(x):
    return jax.nn.sigmoid(x)

def _layernorm(x, axis=-1, eps=1e-05):
    m = jnp.mean(x, axis=axis, keepdims=True)
    v = jnp.var(x, axis=axis, keepdims=True)
    return (x - m) / jnp.sqrt(v + eps)

def _scatter_add(tgt, idx, src, axis=0):
    return tgt.at[idx].add(src)

def _segment_sum(src, seg, n):
    return jax.ops.segment_sum(src, seg, n)
kernel_name = 'mk_seq_preln_d1_jaxref_r4_7b3357'

def setup_inputs(seed: int=0):
    np.random.seed(seed)
    _w = jnp.asarray

    def _L0_attn_setup():
        import jax, jax.numpy as jnp
        import numpy as np
        import math
        HIDDEN = 512
        NUM_HEADS = 16
        HEAD_SIZE = HIDDEN // NUM_HEADS
        BATCH = 2
        SEQ = 512
        key = jax.random.key(seed)
        k_x, k_wq, k_bq, k_wo, k_bo = jax.random.split(key, 5)
        scale_in = 1.0 / math.sqrt(HIDDEN)
        return {'x': jax.random.normal(k_x, (BATCH, SEQ, HIDDEN), dtype=jnp.float32), 'Wqkv': jax.random.normal(k_wq, (HIDDEN, 3 * HIDDEN), dtype=jnp.float32) * scale_in, 'bqkv': jax.random.normal(k_bq, (3 * HIDDEN,), dtype=jnp.float32) * 0.01, 'Wo': jax.random.normal(k_wo, (HIDDEN, HIDDEN), dtype=jnp.float32) * scale_in, 'bo': jax.random.normal(k_bo, (HIDDEN,), dtype=jnp.float32) * 0.01}
    _L0_attn_in = _L0_attn_setup()

    def _L0_ffn_setup():
        import math
        import jax, jax.numpy as jnp
        import numpy as np
        from jax import lax
        D = 512
        I = 256
        E = 32
        K = 4
        NG = 8
        TKG = 3
        NSH = 2
        SCALE = 2.5
        CF = 1.25
        B, S = (2, 512)

        def _router(x, router_w, e_bias):
            scores = jax.nn.sigmoid(x @ router_w.T)
            sc = scores + e_bias[None, :]
            T = x.shape[0]
            gs = sc.reshape(T, NG, E // NG)
            group_scores = lax.top_k(gs, 2)[0].sum(-1)
            _, gidx = lax.top_k(group_scores, TKG)
            gmask = jnp.zeros((T, NG), sc.dtype).at[jnp.arange(T)[:, None], gidx].set(1.0)
            smask = jnp.repeat(gmask, E // NG, axis=1)
            masked = jnp.where(smask > 0, sc, 0.0)
            _, topk_idx = lax.top_k(masked, K)
            topk_w = jnp.take_along_axis(scores, topk_idx, axis=1)
            topk_w = topk_w / (topk_w.sum(-1, keepdims=True) + 1e-20)
            topk_w = topk_w * SCALE
            return (topk_idx.astype(jnp.int32), topk_w)

        def _moe_forward(hidden_states, router_w, e_bias, W_gate, W_up, W_down, shared_gate, shared_up, shared_down):
            b, s, d = hidden_states.shape
            T = b * s
            C = int(math.ceil(CF * T / E))
            EC = E * C
            x = hidden_states.reshape(T, d)
            topk_idx, topk_w = _router(x, router_w, e_bias)
            expert_flat = topk_idx.reshape(-1)
            w_flat = topk_w.reshape(-1)
            tok_flat = jnp.repeat(jnp.arange(T, dtype=jnp.int32), K)
            sort_ix = jnp.argsort(expert_flat)
            e_sorted = expert_flat[sort_ix]
            tok_s = tok_flat[sort_ix]
            w_s = w_flat[sort_ix]
            counts = jnp.zeros(E, jnp.int32).at[e_sorted].add(1)
            group_start = jnp.concatenate([jnp.zeros(1, jnp.int32), jnp.cumsum(counts)[:-1].astype(jnp.int32)])
            pos = jnp.arange(T * K, dtype=jnp.int32) - group_start[e_sorted]
            valid = pos < C
            dest = e_sorted * C + jnp.where(valid, pos, 0)
            slots_token = jnp.zeros(EC, jnp.int32).at[dest].add(jnp.where(valid, tok_s, 0))
            slots_w = jnp.zeros(EC, w_s.dtype).at[dest].add(jnp.where(valid, w_s, 0.0))
            Xp = x[slots_token].reshape(E, C, d)
            G = jnp.einsum('ecd,edi->eci', Xp, W_gate)
            U = jnp.einsum('ecd,edi->eci', Xp, W_up)
            Y = jnp.einsum('eci,eid->ecd', jax.nn.silu(G) * U, W_down)
            Yf = Y.reshape(EC, d) * slots_w[:, None]
            out = jnp.zeros((T, d), x.dtype).at[slots_token].add(Yf)
            shared = jax.nn.silu(x @ shared_gate.T) * (x @ shared_up.T) @ shared_down.T
            return (out + shared).reshape(b, s, d)
        key = jax.random.key(seed)
        ks = jax.random.split(key, 8)

        def rn(k, shape, scale=0.02):
            return jax.random.normal(k, shape, jnp.float32) * scale
        return {'hidden_states': jax.random.normal(ks[0], (B, S, D), jnp.float32), 'router_w': rn(ks[1], (E, D)), 'e_bias': jnp.zeros((E,), jnp.float32), 'W_gate': rn(ks[2], (E, D, I)), 'W_up': rn(ks[3], (E, D, I)), 'W_down': rn(ks[4], (E, I, D)), 'shared_gate': rn(ks[5], (I * NSH, D)), 'shared_up': rn(ks[6], (I * NSH, D)), 'shared_down': rn(ks[7], (D, I * NSH))}
    _L0_ffn_in = _L0_ffn_setup()
    _d = {'L0_attn_x': _L0_attn_in['x'], 'L0_attn_Wqkv': _L0_attn_in['Wqkv'], 'L0_attn_bqkv': _L0_attn_in['bqkv'], 'L0_attn_Wo': _L0_attn_in['Wo'], 'L0_attn_bo': _L0_attn_in['bo'], 'L0_ffn_router_w': _L0_ffn_in['router_w'], 'L0_ffn_e_bias': _L0_ffn_in['e_bias'], 'L0_ffn_W_gate': _L0_ffn_in['W_gate'], 'L0_ffn_W_up': _L0_ffn_in['W_up'], 'L0_ffn_W_down': _L0_ffn_in['W_down'], 'L0_ffn_shared_gate': _L0_ffn_in['shared_gate'], 'L0_ffn_shared_up': _L0_ffn_in['shared_up'], 'L0_ffn_shared_down': _L0_ffn_in['shared_down']}
    _x0 = _d['L0_attn_x']
    _d['L0_attn_x'] = jax.random.normal(jax.random.fold_in(jax.random.key(seed), 1), (16, 512, 512), dtype=_x0.dtype)
    del _x0
    return _d

def reference(L0_attn_x, L0_attn_Wqkv, L0_attn_bqkv, L0_attn_Wo, L0_attn_bo, L0_ffn_router_w, L0_ffn_e_bias, L0_ffn_W_gate, L0_ffn_W_up, L0_ffn_W_down, L0_ffn_shared_gate, L0_ffn_shared_up, L0_ffn_shared_down):

    def _L0_attn_ref(x, Wqkv, bqkv, Wo, bo):
        import jax, jax.numpy as jnp
        import numpy as np
        import math
        HIDDEN = 512
        NUM_HEADS = 16
        HEAD_SIZE = HIDDEN // NUM_HEADS
        BATCH = 2
        SEQ = 512
        b, s, _ = x.shape
        kqv = x @ Wqkv + bqkv
        kqv = kqv.reshape(b, s, 3, NUM_HEADS, HEAD_SIZE)
        q = kqv[:, :, 0]
        k = kqv[:, :, 1]
        v = kqv[:, :, 2]
        scores = jnp.einsum('bsnh,btnh->bnst', k, q) / math.sqrt(HEAD_SIZE)
        ones = jnp.ones_like(scores)
        scores = jnp.triu(scores) + -10000.0 * jnp.tril(ones, k=-1)
        attn = jax.nn.softmax(scores, axis=2)
        out = jnp.einsum('bnkq,bknh->bqnh', attn, v)
        out = out.reshape(b, s, NUM_HEADS * HEAD_SIZE)
        return out @ Wo + bo

    def _L0_ffn_ref(hidden_states, router_w, e_bias, W_gate, W_up, W_down, shared_gate, shared_up, shared_down):
        import math
        import jax, jax.numpy as jnp
        import numpy as np
        from jax import lax
        D = 512
        I = 256
        E = 32
        K = 4
        NG = 8
        TKG = 3
        NSH = 2
        SCALE = 2.5
        CF = 1.25
        B, S = (2, 512)

        def _router(x, router_w, e_bias):
            scores = jax.nn.sigmoid(x @ router_w.T)
            sc = scores + e_bias[None, :]
            T = x.shape[0]
            gs = sc.reshape(T, NG, E // NG)
            group_scores = lax.top_k(gs, 2)[0].sum(-1)
            _, gidx = lax.top_k(group_scores, TKG)
            gmask = jnp.zeros((T, NG), sc.dtype).at[jnp.arange(T)[:, None], gidx].set(1.0)
            smask = jnp.repeat(gmask, E // NG, axis=1)
            masked = jnp.where(smask > 0, sc, 0.0)
            _, topk_idx = lax.top_k(masked, K)
            topk_w = jnp.take_along_axis(scores, topk_idx, axis=1)
            topk_w = topk_w / (topk_w.sum(-1, keepdims=True) + 1e-20)
            topk_w = topk_w * SCALE
            return (topk_idx.astype(jnp.int32), topk_w)

        def _moe_forward(hidden_states, router_w, e_bias, W_gate, W_up, W_down, shared_gate, shared_up, shared_down):
            b, s, d = hidden_states.shape
            T = b * s
            C = int(math.ceil(CF * T / E))
            EC = E * C
            x = hidden_states.reshape(T, d)
            topk_idx, topk_w = _router(x, router_w, e_bias)
            expert_flat = topk_idx.reshape(-1)
            w_flat = topk_w.reshape(-1)
            tok_flat = jnp.repeat(jnp.arange(T, dtype=jnp.int32), K)
            sort_ix = jnp.argsort(expert_flat)
            e_sorted = expert_flat[sort_ix]
            tok_s = tok_flat[sort_ix]
            w_s = w_flat[sort_ix]
            counts = jnp.zeros(E, jnp.int32).at[e_sorted].add(1)
            group_start = jnp.concatenate([jnp.zeros(1, jnp.int32), jnp.cumsum(counts)[:-1].astype(jnp.int32)])
            pos = jnp.arange(T * K, dtype=jnp.int32) - group_start[e_sorted]
            valid = pos < C
            dest = e_sorted * C + jnp.where(valid, pos, 0)
            slots_token = jnp.zeros(EC, jnp.int32).at[dest].add(jnp.where(valid, tok_s, 0))
            slots_w = jnp.zeros(EC, w_s.dtype).at[dest].add(jnp.where(valid, w_s, 0.0))
            Xp = x[slots_token].reshape(E, C, d)
            G = jnp.einsum('ecd,edi->eci', Xp, W_gate)
            U = jnp.einsum('ecd,edi->eci', Xp, W_up)
            Y = jnp.einsum('eci,eid->ecd', jax.nn.silu(G) * U, W_down)
            Yf = Y.reshape(EC, d) * slots_w[:, None]
            out = jnp.zeros((T, d), x.dtype).at[slots_token].add(Yf)
            shared = jax.nn.silu(x @ shared_gate.T) * (x @ shared_up.T) @ shared_down.T
            return (out + shared).reshape(b, s, d)
        return _moe_forward(hidden_states, router_w, e_bias, W_gate, W_up, W_down, shared_gate, shared_up, shared_down)
    x = L0_attn_x
    x = x + _L0_attn_ref(_layernorm(x, axis=-1), L0_attn_Wqkv, L0_attn_bqkv, L0_attn_Wo, L0_attn_bo)
    x = x + _L0_ffn_ref(_layernorm(x, axis=-1), L0_ffn_router_w, L0_ffn_e_bias, L0_ffn_W_gate, L0_ffn_W_up, L0_ffn_W_down, L0_ffn_shared_gate, L0_ffn_shared_up, L0_ffn_shared_down)
    return x

_drawn_inputs = setup_inputs


def setup_inputs(seed=0):
    import zlib

    import numpy as np

    out = dict(_drawn_inputs(seed))
    spreads = {'L0_ffn_e_bias': (0.0, 0.326)}
    factors = {'L0_attn_bqkv': 5.505,
     'L0_attn_bo': 5.573,
     'L0_ffn_router_w': 3.02,
     'L0_ffn_W_gate': 2.818,
     'L0_ffn_W_up': 2.756,
     'L0_ffn_W_down': 2.758}
    for name, (base, spread) in spreads.items():
        noise = np.random.default_rng([zlib.crc32(name.encode()), seed]).standard_normal(out[name].shape)
        drawn = base * np.exp(spread * noise) if base else spread * noise
        out[name] = jnp.asarray(drawn.astype(out[name].dtype))
    for name, factor in factors.items():
        out[name] = (out[name] * factor).astype(out[name].dtype)
    return out
```

```python
from contextlib import ExitStack

import numpy as np

import concourse.bass as bass
from concourse import mybir

F32 = mybir.dt.float32
I32 = mybir.dt.int32
ALU = mybir.AluOpType
ACT = mybir.ActivationFunctionType
AX = mybir.AxisListType

P = 128
BATCH, SEQ, D = 16, 512, 512
TOKENS = BATCH * SEQ
TT = SEQ // P
DK = D // P
HEADS, HD = 16, 32
GH = P // HD
HG = HEADS // GH
STEPS = HG * TT
SCALE = float(HD) ** -0.5
MASKED = -10000.0 / SCALE
EPS = 1e-5
I2 = 512
IB = I2 // P
E, TOPK, NG, TOPG = 32, 4, 8, 3
GE = E // NG
ROUTE_SCALE = 2.5
CAP = (5 * TOKENS // 4 + E - 1) // E
CS = -(-CAP // P)
CAPP = CS * P
LASTC = CAP - (CS - 1) * P
SLOTS = E * CAPP
IE = 256
JB = IE // P
LOW, HIGH = -3.0e38, 3.0e38

GROUPS = ([("out", t, 4) for t in range(TT)] + [("xT", t, 1) for t in range(TT)]
          + [(w, g, 4) for g in range(HG) for w in ("q", "k")] + [("v", t, 4) for t in range(TT)]
          + [("x2T", t, 1) for t in range(TT)] + [("router", 0, 4)]
          + [(w, j, 4) for j in range(IB) for w in ("gate", "up")] + [("pos", 0, 1)]
          + [("down", t, 4) for t in range(TT)])
PROJ = ("xT", "q", "k", "v")
N_PROJ = sum(k in PROJ for k, _, _ in GROUPS)
N_TAIL = len(GROUPS) - N_PROJ
SLOTS_STEP = 8


def schedule(proj, tail):
    out, counts, at = [], {True: 0, False: 0}, 0
    for kind, n, pieces in GROUPS:
        of_proj = kind in PROJ
        if (proj if of_proj else tail):
            out.append((kind, n, at, pieces, len(out), counts[of_proj]))
            counts[of_proj] += 1
        at += pieces
    assert at <= STEPS * SLOTS_STEP and len(out) % 2 == 0
    return out


def setup(nc, a, c, ps):
    with ExitStack() as ctx:
        sem = lambda n: ctx.enter_context(nc.semaphore(n))
        loaded = [sem(f"setup_loaded{i}") for i in range(5)]
        direct_loaded = sem("setup_direct_loaded")
        zeroed = sem("setup_zeroed")
        filled = sem("setup_filled")
        made = sem("setup_made")
        tables_written = sem("setup_tables_written")
        tr_done = sem("setup_tr_done")
        bank_free = [sem("setup_bank_free0"), sem("setup_bank_free1")]
        block = ctx.enter_context(nc.Block())
        raw = [c["qT0"], c["kT0"], c["v0"]]
        dst = [c["sgT"], c["suT"], c["sdT"]]
        rw_raw = c["hT"][0:E, 0, :]
        bqk_raw = c["hT"][0:2 * HG, 1, 0:P]
        jobs = [(w, k) for w in range(3) for k in range(DK)] + [(3, 0), (4, 0)]

        @block.sync
        def _(sp):
            for w, name in enumerate(("shared_gate", "shared_up", "shared_down")):
                sp.dma_start(raw[w][:, :, :], a[name].rearrange("(i p) d -> p i d", p=P)).then_inc(loaded[w], 16)
            sp.dma_start(rw_raw, a["router_w"]).then_inc(loaded[3], 16)
            sp.dma_start(bqk_raw, a["bqkv"][0:2 * D].rearrange("(f p) -> f p", p=P)).then_inc(loaded[4], 16)
            direct = [
                (c["wqkv"][:, :, :], a["Wqkv"].rearrange("(k p) n -> p k n", p=P)),
                (c["wo"][:, :, :], a["Wo"].rearrange("(k p) n -> p k n", p=P)),
                (c["bv"][:, :], a["bqkv"][2 * D:3 * D].rearrange("(o n) -> o n", o=1).broadcast_to([P, D])),
                (c["bo"][:, :], a["bo"].rearrange("(o n) -> o n", o=1).broadcast_to([P, D])),
                (c["ebias"][:, :], a["e_bias"].rearrange("(o n) -> o n", o=1).broadcast_to([P, E])),
            ]
            for to, of in direct:
                sp.dma_start(to, of).then_inc(direct_loaded, 16)
            sp.wait_ge(direct_loaded, 16 * len(direct))
            sp.wait_ge(filled, 2)
            sp.dma_start(a["slots"].rearrange("(e s) w -> e (s w)", e=E),
                         c["S"][0:E, 0:2, :].rearrange("e a n -> e (a n)")[:, 0:2 * CAPP]).then_inc(tables_written, 16)
            for name in ("x2n", "out"):
                for n in range(CS):
                    sp.dma_start(a[name][TOKENS + n * P:TOKENS + (n + 1) * P, :], c["S"][:, 2, :]).then_inc(tables_written, 16)
            sp.wait_ge(tables_written, 16 * (1 + 2 * CS))

        @block.gpsimd
        def _(pool):
            z = pool.memset(c["ident"][:, :], 0.0)
            pool.memset(c["maskrow"][:, :], 0.0)
            pool.memset(c["before"][:, :], 1.0)
            pool.memset(c["ones"][:, :], 1.0)
            pool.memset(c["half"][:, :], -0.5)
            pool.memset(c["carry"][:, :], 0.0)
            pool.memset(c["gval"][:, :, :], LOW)
            pool.memset(c["grep"][:, :, :], LOW)
            pool.memset(c["mval"][:, :, :], LOW)
            pool.memset(c["erep"][:, :, :], LOW)
            pool.memset(c["S"][:, :, :], 0.0).then_inc(zeroed, 1)
            pool.wait_ge(zeroed, 1)
            pool.affine_select(out=c["ident"][:, :], in_=c["ident"][:, :], compare_op=ALU.not_equal, fill=1.0,
                               base=0, pattern=[[-1, P]], channel_multiplier=1)
            tri = c["maskrow"][:, SEQ - P:SEQ]
            pool.affine_select(out=tri, in_=tri, compare_op=ALU.is_ge, fill=MASKED,
                               base=0, pattern=[[-1, P]], channel_multiplier=1)
            pool.affine_select(out=c["before"][:, :], in_=c["before"][:, :], compare_op=ALU.is_gt, fill=0.0,
                               base=0, pattern=[[1, P]], channel_multiplier=-1)
            pool.iota(c["tok_i"][:, :], pattern=[[P, TT]], base=0, channel_multiplier=1)
            pool.iota(c["eoff_i"][:, :, :], pattern=[[0, TT], [CAPP, E]], base=1, channel_multiplier=0)
            pool.iota(c["fill_i"], pattern=[[P, CS], [1, P]], base=TOKENS, channel_multiplier=0).then_inc(made, 1)

        @block.vector
        def _(dve):
            dve.wait_ge(made, 1)
            dve.tensor_copy(c["tok"][:, :], c["tok_i"][:, :])
            dve.tensor_copy(c["eoff"][:, :, :], c["eoff_i"][:, :, :]).then_inc(filled, 1)
            empty = c["S"][0:E, 0:2, :].rearrange("e a n -> e (a n)")[:, 0:2 * CAPP].rearrange("e (s w) -> e s w", w=2)
            dve.tensor_copy(empty[:, :, 0], c["fill_i"].rearrange("e c p -> e (c p)")).then_inc(filled, 1)
            for n, (w, k) in enumerate(jobs):
                dve.wait_ge(tr_done, n + 1)
                if w < 3:
                    dve.tensor_copy(dst[w][:, k, :], ps["dense"][n % 2][:, :]).then_inc(bank_free[n % 2], 1)
                elif w == 4:
                    dve.tensor_copy(c["bqk"][:, :], ps["dense"][n % 2][:, 0:2 * HG]).then_inc(bank_free[n % 2], 1)
                else:
                    dve.tensor_copy(c["rwT"][:, :, :], ps["dense"][n % 2][:, 0:DK * E].rearrange("p (k e) -> p k e", k=DK)
                                    ).then_inc(bank_free[n % 2], 1)

        @block.tensor
        def _(pe):
            pe.wait_ge(made, 1)
            for n, (w, k) in enumerate(jobs):
                if k == 0:
                    pe.wait_ge(loaded[w], 16)
                if n >= 2:
                    pe.wait_ge(bank_free[n % 2], n // 2)
                bank = ps["dense"][n % 2]
                for i in range(4 if w < 4 else 1):
                    if w == 4:
                        last = pe.transpose(bank[:, 0:2 * HG], bqk_raw, c["ident"][0:2 * HG, 0:2 * HG])
                    elif w < 3:
                        last = pe.transpose(bank[:, i * P:(i + 1) * P], raw[w][:, i, k * P:(k + 1) * P], c["ident"][:, :])
                    else:
                        last = pe.transpose(bank[:, i * E:(i + 1) * E], rw_raw[:, i * P:(i + 1) * P], c["ident"][0:E, 0:E])
                last.then_inc(tr_done, 1)


def sequences(nc, a, c, ps):
    with ExitStack() as ctx:
        sem = lambda n: ctx.enter_context(nc.semaphore(n))
        xin_loaded, xres_loaded = sem("xin_loaded"), sem("xres_loaded")
        x2n_stored, out_stored = sem("x2n_stored"), sem("out_stored")
        slots_scattered = sem("slots_scattered")
        proj_done, tail_done = sem("proj_done"), sem("tail_done")
        x1_ready, gate_used, pos_used = sem("x1_ready"), sem("gate_used"), sem("pos_used")
        xT_ready, qk_ready, v_ready, x2T_ready = sem("xT_ready"), sem("qk_ready"), sem("v_ready"), sem("x2T_ready")
        tanh_ready, h_ready = sem("tanh_ready"), sem("h_ready")
        scores_done, masked_done, exp_done = sem("scores_done"), sem("masked_done"), sem("exp_done")
        pT_done, pT_copied, rden_ready = sem("pT_done"), sem("pT_copied"), sem("rden_ready")
        o_done, o_used = sem("o_done"), sem("o_used")
        ln1_stats, ln1_normed = sem("ln1_stats"), sem("ln1_normed")
        ln2_stats, ln2_normed = sem("ln2_stats"), sem("ln2_normed")
        rstd1_ready, rstd2_ready = sem("rstd1_ready"), sem("rstd2_ready")
        xres_biased, out_ready = sem("xres_biased"), sem("out_ready")
        sig_exp, sel_ready, dest_ready = sem("sig_exp"), sem("sel_ready"), sem("dest_ready")
        dve_chain, settled = sem("dve_chain"), sem("settled")
        block = ctx.enter_context(nc.Block())

        x_v = a["x"].rearrange("b (t p) d -> b p t d", p=P)
        x2n_v = a["x2n"][0:TOKENS, :].rearrange("(b t p) d -> b p t d", b=BATCH, p=P)
        out_v = a["out"][0:TOKENS, :].rearrange("(b t p) d -> b p t d", b=BATCH, p=P)

        def turns(eng, turn):
            turn(0, 0, True, False, False)
            turn(1, 1, True, True, False)
            with eng.Fori(0, (BATCH - 2) // 2) as pair:
                turn(pair * 2 + 2, 0, True, True, True)
                turn(pair * 2 + 3, 1, True, True, True)
            turn(BATCH, 0, False, True, True)
            turn(BATCH + 1, 1, False, False, True)

        def settle(eng):
            eng.sem_inc(settled, 1)

        def done_wait(eng, i, kind, at):
            if kind in PROJ:
                eng.wait_ge(proj_done, i * N_PROJ + at + 1)
            else:
                eng.wait_ge(tail_done, (i - 2) * N_TAIL + at + 1)

        def read_wait(eng, i, kind, m):
            b = i - 2
            if kind == "out":
                eng.wait_ge(x1_ready, b * TT + m + 1)
            elif kind == "xT":
                eng.wait_ge(xT_ready, i * TT + m + 1)
            elif kind in ("q", "k"):
                eng.wait_ge(qk_ready, i * 2 * HG + 2 * m + (kind == "k") + 1)
            elif kind == "v":
                eng.wait_ge(v_ready, i * TT + m + 1)
            elif kind == "x2T":
                eng.wait_ge(x2T_ready, b * TT + m + 1)
            elif kind == "router":
                eng.wait_ge(sig_exp, b + 1)
            elif kind == "gate":
                eng.wait_ge(gate_used, b * IB + m + 1)
            elif kind == "up":
                eng.wait_ge(h_ready, b * IB + m + 1)
            elif kind == "pos":
                eng.wait_ge(pos_used, b + 1)
            elif kind == "down":
                eng.wait_ge(out_ready, (b + 1) * TT + m + 1)

        @block.sync
        def _(sp):
            def turn(i, par, proj, attn, fin):
                b = i - 2
                if proj:
                    if not (isinstance(i, int) and i == 0):
                        sp.wait_ge(proj_done, (i - 1) * N_PROJ + TT)
                    sp.dma_start(c["xin"][:, :, :], x_v[i]).then_inc(xin_loaded, 16)
                if attn:
                    if fin:
                        sp.wait_ge(xres_biased, (i - 1) * TT)
                        settle(sp)
                    sp.dma_start(c["xres"][1 - par][:, :, :], x_v[i - 1]).then_inc(xres_loaded, 16)
                if fin:
                    sp.wait_ge(ln2_normed, (b + 1) * TT)
                    sp.dma_start(x2n_v[b], c["x2n"][:, :, :]).then_inc(x2n_stored, 16)
                    sp.wait_ge(out_ready, (b + 2) * TT)
                    sp.dma_start(out_v[b], c["xres"][par][:, :, :]).then_inc(out_stored, 16)
                    sp.wait_ge(out_stored, (b + 1) * 16)
                    settle(sp)

            turns(sp, turn)
            sp.wait_ge(x2n_stored, 16 * BATCH)
            sp.wait_ge(out_stored, 16 * BATCH)

        @block.tensor
        def _(pe):
            ident = c["ident"][:, :]

            def dense(i, par, slot, groups, fin):
                hit = [g for g in groups if g[2] <= slot < g[2] + g[3]]
                if not hit:
                    return
                kind, m, first, pieces, pos, at = hit[0]
                k, b = slot - first, i - 2
                bank = ps["dense"][pos % 2]
                if k == 0 and pos >= 2:
                    read_wait(pe, i, *groups[pos - 2][0:2])
                elif k == 0 and not (isinstance(i, int) and i == 0):
                    pe.wait_ge(v_ready, min(i, BATCH) * TT if isinstance(i, int) else i * TT)
                    if fin:
                        pe.wait_ge(out_ready, (b + 1) * TT)
                blk = slice(m * P, (m + 1) * P)
                if kind == "out":
                    if k == 0:
                        pe.wait_ge(o_used, b * STEPS + STEPS - TT + m + 1)
                    last = pe.matmul(bank[:, :], c["aT"][par][:, k, blk], c["wo"][:, k, :], start=k == 0, stop=k == DK - 1)
                elif kind == "xT":
                    pe.wait_ge(ln1_normed, i * TT + m + 1)
                    for j in range(DK):
                        last = pe.transpose(bank[:, j * P:(j + 1) * P], c["xin"][:, m, j * P:(j + 1) * P], ident)
                elif kind in ("q", "k"):
                    if k == 0 and kind == "q" and m == 0:
                        pe.wait_ge(xT_ready, (i + 1) * TT)
                    off = (kind == "k") * D + m * P
                    last = pe.matmul(bank[:, :], c["wqkv"][:, k, off:off + P], c["xT"][:, k, :], start=k == 0, stop=k == DK - 1)
                elif kind == "v":
                    last = pe.matmul(bank[:, :], c["xT"][:, k, blk], c["wqkv"][:, k, 2 * D:3 * D], start=k == 0, stop=k == DK - 1)
                elif kind == "x2T":
                    pe.wait_ge(ln2_normed, b * TT + m + 1)
                    for j in range(DK):
                        last = pe.transpose(bank[:, j * P:(j + 1) * P], c["x2n"][:, m, j * P:(j + 1) * P], ident)
                elif kind == "router":
                    if k == 0:
                        pe.wait_ge(x2T_ready, (b + 1) * TT)
                    for j in range(DK):
                        last = pe.matmul(bank[:, k * E:(k + 1) * E], c["xT"][:, j, k * P:(k + 1) * P], c["rwT"][:, j, :],
                                         start=j == 0, stop=j == DK - 1)
                elif kind in ("gate", "up"):
                    w = c["sgT"] if kind == "gate" else c["suT"]
                    last = pe.matmul(bank[:, :], w[:, k, blk], c["xT"][:, k, :], start=k == 0, stop=k == DK - 1)
                elif kind == "pos":
                    pe.wait_ge(sel_ready, b + 1)
                    sel = c["sel"][:, :, :].rearrange("p t e -> p (t e)")
                    n = TT * E
                    pe.matmul(bank[:, 0:n], c["ones"][:, :], c["carry4"][:, :, :].rearrange("p t e -> p (t e)"), start=True, stop=False)
                    pe.matmul(bank[:, 0:n], c["before"][:, :], sel, start=False, stop=False)
                    for s in range(1, TT):
                        last = pe.matmul(bank[:, s * E:n], c["ones"][:, :], sel[:, 0:n - s * E], start=False, stop=s == TT - 1)
                elif kind == "down":
                    if m == 0:
                        pe.wait_ge(h_ready, b * IB + k + 1)
                    last = pe.matmul(bank[:, :], c["hT"][:, k, blk], c["sdT"][:, k, :], start=k == 0, stop=k == IB - 1)
                if k == pieces - 1:
                    last.then_inc(proj_done if kind in PROJ else tail_done, 1)

            def scores(i, par, s):
                hg, qt = divmod(s, TT)
                g = (i - 1) * STEPS + s
                if s == 0:
                    pe.wait_ge(qk_ready, i * 2 * HG)
                if not (isinstance(i, int) and i == 1 and s == 0):
                    pe.wait_ge(masked_done, g * GH)
                for h in range(GH):
                    rows = slice(h * HD, (h + 1) * HD)
                    last = pe.matmul(ps["scores"][h][:, 0:(qt + 1) * P], c["qT"][par][rows, hg, qt * P:(qt + 1) * P],
                                     c["kT"][par][rows, hg, 0:(qt + 1) * P], start=True, stop=True)
                last.then_inc(scores_done, 1)

            def transpose_probs(i, s, h):
                g = (i - 1) * STEPS + s
                pe.wait_ge(exp_done, g * GH + h + 1)
                if not (isinstance(i, int) and i == 1 and s == 0 and h == 0):
                    pe.wait_ge(pT_copied, g * GH + h)
                for kt in range(s % TT + 1):
                    last = pe.transpose(ps["pT"][:, kt * P:(kt + 1) * P], c["S"][:, h, kt * P:(kt + 1) * P], ident)
                last.then_inc(pT_done, 1)

            def values(i, par, s):
                hg, qt = divmod(s, TT)
                g = (i - 1) * STEPS + s
                if s == 0:
                    pe.wait_ge(v_ready, i * TT)
                pe.wait_ge(pT_copied, (g + 1) * GH)
                if not (isinstance(i, int) and i == 1 and s == 0):
                    pe.wait_ge(o_used, g)
                for kt in range(qt + 1):
                    for h in range(GH):
                        rows = slice(h * HD, (h + 1) * HD)
                        pe.matmul(ps["o"][rows, 0:P], c["v"][par][:, kt, hg * P + h * HD:hg * P + (h + 1) * HD],
                                  c["pT"][:, h, kt * P:(kt + 1) * P], start=kt == 0, stop=kt == qt)
                pe.wait_ge(rden_ready, g + 1)
                pe.transpose(ps["o"][:, P:2 * P], c["rden"][:, :, :].rearrange("p h d -> p (h d)"), ident).then_inc(o_done, 1)

            def turn(i, par, proj, attn, fin):
                groups = schedule(proj, fin)
                for s in range(STEPS):
                    slot = s * SLOTS_STEP
                    if attn:
                        scores(i, 1 - par, s)
                    dense(i, par, slot, groups, fin)
                    if s == 0 and fin:
                        values(i - 1, par, STEPS - 1)
                    if s > 0 and attn:
                        values(i, 1 - par, s - 1)
                    dense(i, par, slot + 1, groups, fin)
                    dense(i, par, slot + 2, groups, fin)
                    for h in range(GH):
                        if attn:
                            transpose_probs(i, s, h)
                        dense(i, par, slot + 3 + h, groups, fin)
                    dense(i, par, slot + 7, groups, fin)

            turns(pe, turn)

        @block.scalar
        def _(act):
            def copies(i, par, slot, groups):
                hit = [g for g in groups if g[2] + g[3] - 1 == slot]
                if not hit:
                    return
                kind, m, _, _, pos, at = hit[0]
                bank = ps["dense"][pos % 2]
                if kind in ("xT", "x2T"):
                    done_wait(act, i, kind, at)
                    ready = xT_ready if kind == "xT" else x2T_ready
                    act.activation(c["xT"][:, :, m * P:(m + 1) * P], bank[:, :].rearrange("p (k t) -> p k t", k=DK),
                                   ACT.Copy).then_inc(ready, 1)
                elif kind in ("q", "k"):
                    done_wait(act, i, kind, at)
                    f = (kind == "k") * HG + m
                    to = c["qT"] if kind == "q" else c["kT"]
                    act.activation(to[par][:, m, :], bank[:, :], ACT.Identity, bias=c["bqk"][:, f:f + 1]).then_inc(qk_ready, 1)
                elif kind == "router":
                    done_wait(act, i, kind, at)
                    act.activation(c["sig"][:, :, :].rearrange("p t e -> p (t e)"), bank[:, 0:TT * E], ACT.Exp, scale=-1.0).then_inc(sig_exp, 1)
                elif kind == "gate":
                    done_wait(act, i, kind, at)
                    act.activation(c["hT"][:, m, :], bank[:, :], ACT.Tanh, scale=0.5).then_inc(tanh_ready, 1)

            def exp(i, s, h):
                g = (i - 1) * STEPS + s
                row = c["S"][:, h, 0:(s % TT + 1) * P]
                act.wait_ge(masked_done, g * GH + h + 1)
                act.activation(row, row, ACT.Exp, bias=c["nmax"][:, h:h + 1], scale=-1.0,
                               accum_out=c["den"][:, h:h + 1]).then_inc(exp_done, 1)

            def copy_probs(i, s, h):
                g = (i - 1) * STEPS + s
                n = (s % TT + 1) * P
                act.wait_ge(pT_done, g * GH + h + 1)
                act.activation(c["pT"][:, h, 0:n], ps["pT"][:, 0:n], ACT.Copy).then_inc(pT_copied, 1)

            def turn(i, par, proj, attn, fin):
                groups = schedule(proj, fin)
                for s in range(STEPS):
                    slot = s * SLOTS_STEP
                    if attn:
                        exp(i, s, 0)
                        exp(i, s, 1)
                    copies(i, par, slot, groups)
                    if attn:
                        exp(i, s, 2)
                        exp(i, s, 3)
                    copies(i, par, slot + 1, groups)
                    copies(i, par, slot + 2, groups)
                    if attn:
                        copy_probs(i, s, 0)
                    copies(i, par, slot + 3, groups)
                    copies(i, par, slot + 4, groups)
                    if attn:
                        copy_probs(i, s, 2)
                    for n in (5, 6, 7):
                        copies(i, par, slot + n, groups)

            turns(act, turn)

        @block.vector
        def _(dve):
            chain = {"turn": 0, "links": 0}

            def link(ins):
                chain["links"] += 1
                ins.then_inc(dve_chain, 1)
                dve.wait_ge(dve_chain, chain["turn"] + chain["links"])

            def statistics(x, stats, mv):
                link(dve.bn_stats(stats, x))
                settle(dve)
                return dve.bn_aggr(mv, stats)

            def route(i):
                flat = lambda t: t[:, :, :].rearrange("p t e -> p (t e)")
                dve.wait_ge(sig_exp, i - 1)
                link(dve.tensor_scalar_add(flat(c["sig"]), flat(c["sig"]), 1.0))
                link(dve.reciprocal(flat(c["sig"]), flat(c["sig"])))
                link(dve.tensor_tensor(c["sc"][:, :, :], c["sig"][:, :, :], c["ebias"][:, :].unsqueeze(1).broadcast_to([P, TT, E]), ALU.add))
                s4 = flat(c["sc"]).rearrange("p (g e) -> p g e", e=GE)
                hi, lo, m1, m2 = c["hi"][:, :, :], c["lo"][:, :, :], c["m1"][:, :], c["m2"][:, :]
                dve.tensor_tensor(hi, s4[:, :, 0:2], s4[:, :, 2:4], ALU.max)
                link(dve.tensor_tensor(lo, s4[:, :, 0:2], s4[:, :, 2:4], ALU.min))
                dve.tensor_tensor(m1, hi[:, :, 0], hi[:, :, 1], ALU.max)
                dve.tensor_tensor(m2, hi[:, :, 0], hi[:, :, 1], ALU.min)
                link(dve.tensor_tensor(lo[:, :, 0], lo[:, :, 0], lo[:, :, 1], ALU.max))
                link(dve.tensor_tensor(m2, m2, lo[:, :, 0], ALU.max))
                group = lambda t: t.rearrange("p (t g) -> p t g", t=TT)
                link(dve.tensor_tensor(c["gval"][:, :, 0:NG], group(m1), group(m2), ALU.add))
                settle(dve)
                for t in range(TT):
                    last = dve.max(c["top8"][:, t, :], c["gval"][:, t, 0:NG])
                link(last)
                link(dve.tensor_copy(c["grep"][:, :, 0:TOPG], c["top8"][:, :, 0:TOPG]))
                settle(dve)
                for t in range(TT):
                    last = dve.match_replace(c["gout"][:, t, :], c["grep"][:, t, :], c["gval"][:, t, :], HIGH)
                link(last)
                link(dve.tensor_scalar(c["gmask"][:, :, :], c["gout"][:, :, 0:NG], HIGH / 2, None, ALU.is_ge))
                for t in range(TT):
                    last = dve.tensor_tensor(c["mval"][:, t, 0:E].rearrange("p (g e) -> p g e", e=GE),
                                             c["sc"][:, t, :].rearrange("p (g e) -> p g e", e=GE),
                                             c["gmask"][:, t, :].unsqueeze(2).broadcast_to([P, NG, GE]), ALU.mult)
                link(last)
                link(dve.tensor_scalar_add(c["mval"][:, :, 0:E], c["mval"][:, :, 0:E], 0.0))
                settle(dve)
                for t in range(TT):
                    last = dve.max(c["top8"][:, t, :], c["mval"][:, t, 0:E])
                link(last)
                link(dve.tensor_copy(c["erep"][:, :, 0:TOPK], c["top8"][:, :, 0:TOPK]))
                settle(dve)
                for t in range(TT):
                    last = dve.match_replace(c["eout"][:, t, :], c["erep"][:, t, :], c["mval"][:, t, :], HIGH)
                link(last)
                link(dve.tensor_scalar(c["sel"][:, :, :], c["eout"][:, :, 0:E], HIGH / 2, None, ALU.is_ge))
                dve.tensor_copy(c["carry4"][:, :, :], c["carry"][:, :].unsqueeze(1).broadcast_to([P, TT, E])).then_inc(sel_ready, 1)
                link(dve.tensor_tensor(flat(c["wgt"]), flat(c["sig"]), flat(c["sel"]), ALU.mult))
                dve.tensor_reduce(c["count"][:, :], c["sel"][:, :, :].rearrange("p t e -> p e t"), AX.X, ALU.add)
                link(dve.tensor_reduce(c["wsum"][:, :], c["wgt"][:, :, :], AX.X, ALU.add))
                dve.tensor_tensor(c["carry"][:, :], c["carry"][:, :], c["count"][:, :], ALU.add)
                link(dve.tensor_scalar_add(c["wsum"][:, :], c["wsum"][:, :], 1e-20))
                link(dve.reciprocal(c["wsum"][:, :], c["wsum"][:, :]))
                link(dve.tensor_scalar_mul(c["wsum"][:, :], c["wsum"][:, :], ROUTE_SCALE / 2))
                link(dve.tensor_tensor(c["wgt"][:, :, :], c["wgt"][:, :, :], c["wsum"][:, :].unsqueeze(2).broadcast_to([P, TT, E]), ALU.mult))

            def destinations(i, bank, pos):
                flat = lambda t: t[:, :, :].rearrange("p t e -> p (t e)")
                n = TT * E
                dve.scalar_tensor_tensor(flat(c["eout"])[:, 0:n], bank[:, 0:n], float(CAP), flat(c["sel"]), ALU.is_lt, ALU.mult)
                dve.tensor_tensor(flat(c["sc"]), bank[:, 0:n], flat(c["eoff"]), ALU.add).then_inc(pos_used, 1)
                dve.wait_ge(pos_used, i - 1)
                link(dve.tensor_tensor(flat(c["sc"]), flat(c["sc"]), flat(c["eout"])[:, 0:n], ALU.mult))
                settle(dve)
                for t in range(TT):
                    last = dve.max(c["top8"][:, t, :], c["sc"][:, t, :])
                link(last)
                top = c["top8"][:, :, 0:TOPK]
                for t in range(TT):
                    last = dve.tensor_tensor(c["eq"][:, t, :, :], c["sc"][:, t, :].unsqueeze(1).broadcast_to([P, TOPK, E]),
                                             c["top8"][:, t, 0:TOPK].unsqueeze(2).broadcast_to([P, TOPK, E]), ALU.is_equal)
                link(last)
                for t in range(TT):
                    last = dve.tensor_tensor(c["eq"][:, t, :, :], c["eq"][:, t, :, :],
                                             c["wgt"][:, t, :].unsqueeze(1).broadcast_to([P, TOPK, E]), ALU.mult)
                link(last)
                dve.tensor_reduce(c["rec"][:, :, :, 1], c["eq"][:, :, :, :], AX.X, ALU.add)
                dve.tensor_copy(c["rec"][:, :, :, 0], c["tok"][:, :].unsqueeze(2).broadcast_to([P, TT, TOPK]))
                link(dve.tensor_scalar(c["none"][:, :, :], top, 0.5, float(1 << 20), ALU.is_lt, ALU.mult))
                link(dve.scalar_tensor_tensor(c["idxf"][:, :, :], top, -1.0, c["none"][:, :, :], ALU.add, ALU.add))
                link(dve.tensor_copy(c["idx"][:, :, :], c["idxf"][:, :, :]))
                dve.tensor_scalar_add(c["tok"][:, :], c["tok"][:, :], float(SEQ)).then_inc(dest_ready, 1)

            def copies(i, par, slot, groups):
                hit = [g for g in groups if g[2] + g[3] - 1 == slot]
                if not hit:
                    return
                kind, m, _, _, pos, at = hit[0]
                bank, b = ps["dense"][pos % 2], i - 2
                if kind == "out":
                    x1 = c["xres"][par][:, m, :]
                    dve.wait_ge(xres_biased, (b + 1) * TT)
                    done_wait(dve, i, kind, at)
                    dve.tensor_tensor(x1, bank[:, :], x1, ALU.add).then_inc(x1_ready, 1)
                    dve.wait_ge(x1_ready, b * TT + m + 1)
                    statistics(x1, c["stats2"][:, m, :], c["mv2"][:, m, :]).then_inc(ln2_stats, 1)
                elif kind == "v":
                    done_wait(dve, i, kind, at)
                    dve.tensor_tensor(c["v"][par][:, m, :], bank[:, :], c["bv"][:, :], ALU.add).then_inc(v_ready, 1)
                elif kind == "router":
                    route(i)
                elif kind == "gate":
                    dve.wait_ge(tanh_ready, b * IB + m + 1)
                    dve.scalar_tensor_tensor(c["hT"][:, m, :], c["hT"][:, m, :], 1.0, bank[:, :], ALU.add, ALU.mult).then_inc(gate_used, 1)
                elif kind == "up":
                    done_wait(dve, i, kind, at)
                    dve.wait_ge(gate_used, b * IB + m + 1)
                    dve.tensor_tensor(c["hT"][:, m, :], c["hT"][:, m, :], bank[:, :], ALU.mult).then_inc(h_ready, 1)
                elif kind == "pos":
                    done_wait(dve, i, kind, at)
                    destinations(i, bank, pos)
                elif kind == "down":
                    done_wait(dve, i, kind, at)
                    x1 = c["xres"][par][:, m, :]
                    dve.scalar_tensor_tensor(x1, bank[:, :], 0.5, x1, ALU.mult, ALU.add).then_inc(out_ready, 1)

            def mask(i, s, h):
                g = (i - 1) * STEPS + s
                n = (s % TT + 1) * P
                if h == 0:
                    dve.wait_ge(scores_done, g + 1)
                if not (isinstance(i, int) and i == 1 and s == 0):
                    dve.wait_ge(pT_done, (g - 1) * GH + h + 1)
                settle(dve)
                dve.tensor_tensor_reduce(out=c["S"][:, h, 0:n], in0=ps["scores"][h][:, 0:n], in1=c["maskrow"][:, SEQ - n:SEQ],
                                         scale=-SCALE, scalar=HIGH, op0=ALU.add, op1=ALU.min,
                                         accum_out=c["nmax"][:, h:h + 1]).then_inc(masked_done, 1)

            def copy_probs(i, s, h):
                g = (i - 1) * STEPS + s
                n = (s % TT + 1) * P
                dve.wait_ge(pT_done, g * GH + h + 1)
                dve.tensor_copy(c["pT"][:, h, 0:n], ps["pT"][:, 0:n]).then_inc(pT_copied, 1)

            def denominators(i, s):
                g = (i - 1) * STEPS + s
                dve.wait_ge(exp_done, (g + 1) * GH)
                if not (isinstance(i, int) and i == 1 and s == 0):
                    dve.wait_ge(o_done, g)
                dve.reciprocal(c["rden"][:, :, :], c["den"][:, :].unsqueeze(2).broadcast_to([P, GH, HD])).then_inc(rden_ready, 1)

            def normalise(i, par, s):
                hg, qt = divmod(s, TT)
                g = (i - 1) * STEPS + s
                dve.wait_ge(o_done, g + 1)
                link(dve.tensor_copy(c["rdenT"][:, :], ps["o"][:, P:2 * P]))
                dve.tensor_tensor(c["aT"][par][:, hg, qt * P:(qt + 1) * P], ps["o"][:, 0:P], c["rdenT"][:, :], ALU.mult).then_inc(o_used, 1)

            def turn(i, par, proj, attn, fin):
                groups = schedule(proj, fin)
                chain["links"] = 0
                for s in range(STEPS):
                    slot = s * SLOTS_STEP
                    if attn:
                        for h in range(GH):
                            mask(i, s, h)
                    copies(i, par, slot, groups)
                    if s == 0 and fin:
                        normalise(i - 1, par, STEPS - 1)
                    if s > 0 and attn:
                        normalise(i, 1 - par, s - 1)
                    copies(i, par, slot + 1, groups)
                    copies(i, par, slot + 2, groups)
                    if attn:
                        copy_probs(i, s, 1)
                    for n in (3, 4, 5):
                        copies(i, par, slot + n, groups)
                    if attn:
                        copy_probs(i, s, 3)
                        denominators(i, s)
                    for n in (6, 7):
                        copies(i, par, slot + n, groups)
                    if proj and s < 2:
                        for t in (2 * s, 2 * s + 1):
                            if t == 0:
                                dve.wait_ge(xin_loaded, (i + 1) * 16)
                            statistics(c["xin"][:, t, :], c["stats1"][:, t, :], c["mv1"][:, t, :]).then_inc(ln1_stats, 1)
                chain["turn"] += chain["links"]

            def counted(i, par, proj, attn, fin):
                if isinstance(i, int):
                    turn(i, par, proj, attn, fin)
                else:
                    start = chain.setdefault("loop", chain["turn"])
                    chain["turn"] = (i - 2) * LINKS + start
                    turn(i, par, proj, attn, fin)
                    assert chain["links"] == LINKS, chain["links"]
                    chain["turn"] = start + (BATCH - 2) * LINKS

            dve.sem_inc(out_ready, TT)
            turns(dve, counted)

        @block.gpsimd
        def _(pool):
            def norm(x, to, mv, rstd, done, count):
                settle(pool)
                pool.tensor_scalar(mv[:, 1:2], mv[:, 1:2], EPS, None, ALU.add).then_inc(rstd, 1)
                pool.wait_ge(rstd, count * 2 - 1)
                pool.tensor_tensor(mv[:, 1:2], mv[:, 1:2], c["half"][:, :], ALU.pow).then_inc(rstd, 1)
                pool.wait_ge(rstd, count * 2)
                settle(pool)
                pool.tensor_scalar(to, x, mv[:, 0:1], mv[:, 1:2], ALU.subtract, ALU.mult).then_inc(done, 1)

            def turn(i, par, proj, attn, fin):
                b = i - 2
                for t in range(TT):
                    if proj:
                        pool.wait_ge(ln1_stats, i * TT + t + 1)
                        norm(c["xin"][:, t, :], c["xin"][:, t, :], c["mv1"][:, t, :], rstd1_ready, ln1_normed, i * TT + t + 1)
                    if fin:
                        pool.wait_ge(ln2_stats, b * TT + t + 1)
                        norm(c["xres"][par][:, t, :], c["x2n"][:, t, :], c["mv2"][:, t, :], rstd2_ready, ln2_normed, b * TT + t + 1)
                if attn:
                    pool.wait_ge(xres_loaded, (i) * 16)
                    for t in range(TT):
                        xt = c["xres"][1 - par][:, t, :]
                        pool.tensor_tensor(xt, xt, c["bo"][:, :], ALU.add).then_inc(xres_biased, 1)
                if fin:
                    pool.wait_ge(dest_ready, b + 1)
                    settle(pool)
                    for t in range(TT):
                        for k in range(TOPK):
                            pool.indirect_dma_start(
                                out=a["slots"], out_offset=bass.IndirectOffsetOnAxis(ap=c["idx"][:, t, k:k + 1], axis=0),
                                in_=c["rec"][:, t, k, :], in_offset=None, bounds_check=SLOTS - 1,
                                oob_is_err=False).then_inc(slots_scattered, 16)
                    pool.wait_ge(x2n_stored, (b + 1) * 16)
                    settle(pool)
                    pool.wait_ge(slots_scattered, (b + 1) * (TT * TOPK * 16))
                    settle(pool)

            turns(pool, turn)


def experts(nc, a, e_, ps):
    with ExitStack() as ctx:
        sem = lambda n: ctx.enter_context(nc.semaphore(n))
        table_loaded, table_split, table_T, table_ready = sem("table_loaded"), sem("table_split"), sem("table_T"), sem("table_ready")
        idx_ready = sem("idx_ready")
        gathered = [sem("gathered0"), sem("gathered1")]
        w_loaded = [sem("w_loaded0"), sem("w_loaded1")]
        xT_done, xT_copied = sem("ex_xT_done"), sem("ex_xT_copied")
        gu_done, tanh_ready, h_ready = sem("ex_gu_done"), sem("ex_tanh_ready"), sem("ex_h_ready")
        y_done, y_ready, y_added = sem("y_done"), sem("y_ready"), sem("y_added")
        wcol_ready, settled = sem("wcol_ready"), sem("ex_settled")
        block = ctx.enter_context(nc.Block())

        def settle(eng):
            eng.sem_inc(settled, 1)

        rows = lambda ch: P if ch < CS - 1 else LASTC

        def pairs(eng, expert):
            expert(0, 0, True, True)
            expert(1, 1, True, True)
            with eng.Fori(1, E // 2 - 1) as pair:
                expert(pair * 2, 0, False, True)
                expert(pair * 2 + 1, 1, False, True)
            expert(E - 2, 0, False, True)
            expert(E - 1, 1, False, False)

        def use(e, q):
            return (e // 2 + 1) if isinstance(e, int) else None

        @block.sync
        def _(sp):
            sp.dma_start(e_["table"][:, :], a["slots"].rearrange("(r s) w -> r (s w)", s=P)).then_inc(table_loaded, 16)

            def load(e, q):
                sp.dma_start(e_["wg"][q][:, :, :], a["W_gate"].rearrange("e (k p) n -> e p k n", p=P)[e]).then_inc(w_loaded[q], 16)
                sp.dma_start(e_["wu"][q][:, :, :], a["W_up"].rearrange("e (k p) n -> e p k n", p=P)[e]).then_inc(w_loaded[q], 16)
                sp.dma_start(e_["wd"][q][:, :, :], a["W_down"].rearrange("e (j p) n -> e p j n", p=P)[e]).then_inc(w_loaded[q], 16)

            load(0, 0)

            def expert(e, q, first, succ):
                if succ:
                    if not (isinstance(e, int) and e == 0):
                        sp.wait_ge(y_done, e * CS)
                    load(e + 1, 1 - q)

            pairs(sp, expert)

        @block.gpsimd
        def _(pool):
            pool.wait_ge(table_ready, 2)

            def gather(e, q):
                pool.tensor_copy(e_["idx"][q][:, :], e_["tok"][:, bass.ds(e * CS, CS)]).then_inc(idx_ready, 1)
                pool.wait_ge(idx_ready, e + 1)
                settle(pool)
                for ch in range(CS):
                    r = rows(ch)
                    pool.indirect_dma_start(
                        out=e_["xg"][q][0:r, ch, :], out_offset=None, in_=a["x2n"],
                        in_offset=bass.IndirectOffsetOnAxis(ap=e_["idx"][q][0:r, ch:ch + 1], axis=0)).then_inc(gathered[q], 16)

            gather(0, 0)

            def expert(e, q, first, succ):
                if succ:
                    if not (isinstance(e, int) and e == 0):
                        pool.wait_ge(xT_done, e * CS)
                        pool.wait_ge(y_added, e * CS * 16)
                    settle(pool)
                    gather(e + 1, 1 - q)
                pool.wait_ge(y_ready, (e + 1) * CS)
                if not (isinstance(e, int) and e == 0):
                    pool.wait_ge(y_added, e * CS * 16)
                settle(pool)
                for ch in range(CS):
                    r = rows(ch)
                    pool.indirect_dma_start(
                        out=a["out"], out_offset=bass.IndirectOffsetOnAxis(ap=e_["idx"][q][0:r, ch:ch + 1], axis=0),
                        in_=e_["y"][q][0:r, ch, :], in_offset=None, compute_op=ALU.add).then_inc(y_added, 16)

            pairs(pool, expert)
            pool.wait_ge(y_added, E * CS * 16)

        @block.tensor
        def _(pe):
            pe.wait_ge(table_split, 2)
            nr = E * CS
            for w in range(2):
                pe.transpose(ps["scores"][w][:, 0:nr], e_["split"][:, w, :], e_["ident"][0:nr, 0:nr]).then_inc(table_T, 1)

            def transposes(e, q):
                pe.wait_ge(gathered[q], uses[q](e))
                for ch in range(CS):
                    r, m = rows(ch), e * CS + ch
                    if not (isinstance(e, int) and m < 2):
                        pe.wait_ge(xT_copied, m - 1)
                    settle(pe)
                    bank = [ps["pT"], ps["o"]][(q * CS + ch) % 2]
                    for k in range(DK):
                        last = pe.transpose(bank[:, k * P:k * P + r], e_["xg"][q][0:r, ch, k * P:(k + 1) * P], e_["ident"][0:r, 0:r])
                    last.then_inc(xT_done, 1)

            uses = [lambda e: (e + 2) * (CS * 8), lambda e: (e + 1) * (CS * 8)]
            transposes(0, 0)

            def expert(e, q, first, succ):
                pe.wait_ge(w_loaded[q], uses[q](e))
                pe.wait_ge(xT_copied, (e + 1) * CS)
                if not (isinstance(e, int) and e == 0):
                    pe.wait_ge(h_ready, e * 2 * JB)
                for j in range(JB):
                    for n, w in enumerate(("wg", "wu")):
                        for k in range(DK):
                            last = pe.matmul(ps["scores"][2 * j + n][:, 0:CAP], e_[w][q][:, k, j * P:(j + 1) * P],
                                             e_["xT"][:, k, :], start=k == 0, stop=k == DK - 1)
                        last.then_inc(gu_done, 1)
                if succ:
                    transposes(e + 1, 1 - q)
                for ch in range(CS):
                    r, m = rows(ch), e * CS + ch
                    if not (isinstance(e, int) and m < 2):
                        pe.wait_ge(y_ready, m - 1)
                    for j in range(JB):
                        if ch == 0:
                            pe.wait_ge(h_ready, e * 2 * JB + 2 * (j + 1))
                        last = pe.matmul(ps["dense"][(q * CS + ch) % 2][0:r, :], e_["hT"][:, j, ch * P:ch * P + r],
                                         e_["wd"][q][:, j, :], start=j == 0, stop=j == JB - 1)
                    last.then_inc(y_done, 1)

            pairs(pe, expert)

        @block.scalar
        def _(act):
            def copies(e, q):
                for ch in range(CS):
                    r, m = rows(ch), e * CS + ch
                    act.wait_ge(xT_done, m + 1)
                    bank = [ps["pT"], ps["o"]][(q * CS + ch) % 2]
                    act.activation(e_["xT"][:, :, ch * P:ch * P + r], bank[:, :].rearrange("p (k t) -> p k t", k=DK)[:, :, 0:r],
                                   ACT.Copy).then_inc(xT_copied, 1)

            copies(0, 0)

            def expert(e, q, first, succ):
                for j in range(JB):
                    act.wait_ge(gu_done, e * 2 * JB + 2 * j + 1)
                    act.activation(e_["hT"][:, j, :], ps["scores"][2 * j][:, 0:CAP], ACT.Tanh, scale=0.5).then_inc(tanh_ready, 1)
                if succ:
                    copies(e + 1, 1 - q)

            pairs(act, expert)

        @block.vector
        def _(dve):
            dve.wait_ge(table_loaded, 16)
            pairs_v = e_["table"][:, :].rearrange("r (s w) -> r s w", w=2)
            for w in range(2):
                dve.tensor_copy(e_["split"][:, w, :], pairs_v[:, :, w]).then_inc(table_split, 1)
            dve.wait_ge(table_T, 2)
            dve.tensor_copy(e_["tok"][:, :], ps["scores"][0][:, 0:E * CS]).then_inc(table_ready, 1)
            dve.tensor_copy(e_["w"][:, :], ps["scores"][1][:, 0:E * CS]).then_inc(table_ready, 1)
            dve.wait_ge(table_ready, 2)

            def expert(e, q, first, succ):
                dve.tensor_copy(e_["wcol"][q][:, :], e_["w"][:, bass.ds(e * CS, CS)]).then_inc(wcol_ready, 1)
                for j in range(JB):
                    dve.wait_ge(tanh_ready, e * JB + j + 1)
                    h = e_["hT"][:, j, :]
                    dve.scalar_tensor_tensor(h, h, 1.0, ps["scores"][2 * j][:, 0:CAP], ALU.add, ALU.mult).then_inc(h_ready, 1)
                    dve.wait_ge(gu_done, e * 2 * JB + 2 * j + 2)
                    dve.wait_ge(h_ready, e * 2 * JB + 2 * j + 1)
                    dve.tensor_tensor(h, h, ps["scores"][2 * j + 1][:, 0:CAP], ALU.mult).then_inc(h_ready, 1)
                dve.wait_ge(wcol_ready, e + 1)
                if not first:
                    dve.wait_ge(y_added, (e - 1) * CS * 16)
                for ch in range(CS):
                    r, m = rows(ch), e * CS + ch
                    dve.wait_ge(y_done, m + 1)
                    dve.tensor_scalar(e_["y"][q][0:r, ch, :], ps["dense"][(q * CS + ch) % 2][0:r, :],
                                      e_["wcol"][q][0:r, ch:ch + 1], None, ALU.mult).then_inc(y_ready, 1)

            pairs(dve, expert)


LINKS = 54


def transformer_block(nc, a):
    with ExitStack() as ctx:
        def pb(name):
            return ctx.enter_context(nc.psum_tensor(name, [P, 512], F32))

        ps = {"scores": [pb(f"scores{g}") for g in range(GH)], "pT": pb("pT_ps"), "o": pb("o_ps"),
              "dense": [pb("dense0"), pb("dense1")]}
        ident = ctx.enter_context(nc.sbuf_tensor("ident", [P, P], F32))
        with ExitStack() as first:
            def sb(name, shape, dt=F32):
                return first.enter_context(nc.sbuf_tensor(name, shape, dt))

            c = {"ident": ident}
            for n in ("wqkv",):
                c[n] = sb(n, [P, DK, 3 * D])
            for n in ("wo", "sgT", "suT", "sdT", "qT0", "qT1", "kT0", "kT1", "v0", "v1", "xin", "xT", "aT0", "aT1",
                      "xres0", "xres1", "x2n", "hT", "S", "pT"):
                c[n] = sb(n, [P, 4, 512])
            for n in ("qT", "kT", "v", "aT", "xres"):
                c[n] = [c[n + "0"], c[n + "1"]]
            c["rwT"] = sb("rwT", [P, DK, E])
            c["bqk"] = sb("bqk", [P, 2 * HG])
            c["bv"], c["bo"], c["maskrow"] = sb("bv", [P, D]), sb("bo", [P, D]), sb("maskrow", [P, SEQ])
            c["ebias"] = sb("ebias", [P, E])
            c["ones"], c["before"] = sb("ones", [P, P]), sb("before", [P, P])
            c["nmax"], c["den"] = sb("nmax", [P, GH]), sb("den", [P, GH])
            c["rden"], c["rdenT"] = sb("rden", [P, GH, HD]), sb("rdenT", [P, P])
            c["half"] = sb("half", [P, 1])
            c["stats1"], c["stats2"] = sb("stats1", [P, TT, 6]), sb("stats2", [P, TT, 6])
            c["mv1"], c["mv2"] = sb("mv1", [P, TT, 2]), sb("mv2", [P, TT, 2])
            for n in ("sig", "sc", "sel", "wgt", "carry4", "eoff"):
                c[n] = sb(n, [P, TT, E])
            c["hi"], c["lo"] = sb("hi", [P, TT * NG, 2]), sb("lo", [P, TT * NG, 2])
            c["m1"], c["m2"] = sb("m1", [P, TT * NG]), sb("m2", [P, TT * NG])
            c["gval"], c["gout"] = sb("gval", [P, TT, NG + 8 - TOPG]), sb("gout", [P, TT, NG + 8 - TOPG])
            c["mval"], c["eout"] = sb("mval", [P, TT, E + 8 - TOPK]), sb("eout", [P, TT, E + 8 - TOPK])
            c["grep"], c["erep"], c["top8"] = sb("grep", [P, TT, 8]), sb("erep", [P, TT, 8]), sb("top8", [P, TT, 8])
            c["gmask"] = sb("gmask", [P, TT, NG])
            c["carry"], c["count"], c["wsum"] = sb("carry", [P, E]), sb("count", [P, E]), sb("wsum", [P, TT])
            c["eq"] = sb("eq", [P, TT, TOPK, E])
            c["rec"] = sb("rec", [P, TT, TOPK, 2])
            c["none"], c["idxf"], c["idx"] = sb("none", [P, TT, TOPK]), sb("idxf", [P, TT, TOPK]), sb("idx", [P, TT, TOPK], I32)
            c["tok"], c["tok_i"] = sb("tok", [P, TT]), sb("tok_i", [P, TT], I32)
            c["eoff_i"] = c["wgt"][:, :, :].bitcast(I32)
            c["fill_i"] = c["S"][0:E, 3, 0:CAPP].bitcast(I32).rearrange("e (c p) -> e c p", p=P)
            setup(nc, a, c, ps)
            sequences(nc, a, c, ps)
        with ExitStack() as second:
            def sb2(name, shape, dt=F32):
                return second.enter_context(nc.sbuf_tensor(name, shape, dt))

            nr = E * CS
            e_ = {"ident": ident, "table": sb2("table", [nr, 2 * P]), "split": sb2("split", [nr, 2, P]),
                  "tok": sb2("slot_tok", [P, nr], I32), "w": sb2("slot_w", [P, nr]),
                  "xT": sb2("ex_xT", [P, DK, CAP]), "hT": sb2("ex_hT", [P, JB, CAP])}
            for n, shape, dt in (("wg", [P, DK, IE], F32), ("wu", [P, DK, IE], F32), ("wd", [P, JB, D], F32),
                                 ("xg", [P, CS, D], F32), ("y", [P, CS, D], F32), ("idx", [P, CS], I32), ("wcol", [P, CS], F32)):
                e_[n] = [sb2(f"ex_{n}{q}", shape, dt) for q in range(2)]
            experts(nc, a, e_, ps)


_INS = {"x": "L0_attn_x", "Wqkv": "L0_attn_Wqkv", "bqkv": "L0_attn_bqkv", "Wo": "L0_attn_Wo", "bo": "L0_attn_bo",
        "router_w": "L0_ffn_router_w", "e_bias": "L0_ffn_e_bias", "W_gate": "L0_ffn_W_gate", "W_up": "L0_ffn_W_up",
        "W_down": "L0_ffn_W_down", "shared_gate": "L0_ffn_shared_gate", "shared_up": "L0_ffn_shared_up",
        "shared_down": "L0_ffn_shared_down"}


def kernel(**inputs):
    import concourse.bacc as _bacc
    from concourse.bass_utils import run_bass_kernel_spmd as _run

    nc = _bacc.Bacc("TRN2", target_bir_lowering=False, num_devices=1)
    arrays, a = {}, {}
    for short, name in _INS.items():
        arrays[f"in_{short}"] = np.ascontiguousarray(inputs[name])
        a[short] = nc.dram_tensor(f"in_{short}", arrays[f"in_{short}"].shape, F32, kind="ExternalInput").ap()
    a["out"] = nc.dram_tensor("out_0", (TOKENS + CAPP, D), F32, kind="ExternalOutput").ap()
    a["x2n"] = nc.dram_tensor("x2n_dram", (TOKENS + CAPP, D), F32, kind="Internal").ap()
    a["slots"] = nc.dram_tensor("slots_dram", (SLOTS, 2), F32, kind="Internal").ap()
    transformer_block(nc, a)
    r = _run(nc, [arrays], core_ids=[0])
    return np.asarray(r.results[0]["out_0"])[:TOKENS].reshape(BATCH, SEQ, D)
```

```python
from contextlib import ExitStack

import numpy as np

import concourse.bass as bass
from concourse import mybir

F32 = mybir.dt.float32
F16 = mybir.dt.float16
I32 = mybir.dt.int32
ALU = mybir.AluOpType
ACT = mybir.ActivationFunctionType
AX = mybir.AxisListType

P = 128
BATCH, SEQ, D = 16, 512, 512
TOKENS = BATCH * SEQ
TT = SEQ // P
DK = D // P
HEADS, HD = 16, 32
GH = P // HD
HG = HEADS // GH
STEPS = HG * TT
SCALE = float(HD) ** -0.5
MASKED = -10000.0 / SCALE
EPS = 1e-5
I2 = 512
IB = I2 // P
E, TOPK, NG, TOPG = 32, 4, 8, 3
GE = E // NG
ROUTE_SCALE = 2.5
CAP = (5 * TOKENS // 4 + E - 1) // E
CS = -(-CAP // P)
CAPP = CS * P
LASTC = CAP - (CS - 1) * P
SLOTS = E * CAPP
IE = 256
JB = IE // P
WS = 2.0 ** 6
XS = 2.0 ** 10
AS = 2.0 ** 8
HS = 2.0 ** 4
DENSE = 3
LOW, HIGH = -3.0e38, 3.0e38

GROUPS = ([g for t in range(TT) for g in (("xT", t, 1), ("out", t, 4))]
          + [(w, g, 4) for g in range(HG) for w in ("q", "k")]
          + [("v", 0, 4)] + [g for t in range(1, TT) for g in (("v", t, 4), ("x2T", t - 1, 1))]
          + [("x2T", TT - 1, 1), ("router", 0, 4)]
          + [(w, j, 4) for j in range(IB // 2) for w in ("gate", "up")] + [("pos", 0, 1)]
          + [(w, j, 4) for j in range(IB // 2, IB) for w in ("gate", "up")]
          + [("down", t, 4) for t in range(TT)])


def last_slot(kind, n):
    at = 0
    for k, m, pieces in GROUPS:
        at += pieces
        if (k, m) == (kind, n):
            return at - 1


LN2_SLOT = {last_slot("out", t) + 3: t for t in range(TT)}
STAT_SLOT = {last_slot("router", 0) + 9 + 4 * t: t for t in range(TT)}
LN1_SLOT = {slot + 6: t for slot, t in STAT_SLOT.items()}
ROUTE_SLOT = {last_slot("router", 0) + 1 + n: n for n in range(6)}
DEST_SLOT = {last_slot("pos", 0) + at: n for n, at in enumerate((0, 7, 9, 11))}
LAST_H = last_slot("up", IB - 1) + 1
PROJ = ("xT", "q", "k", "v")
N_PROJ = sum(k in PROJ for k, _, _ in GROUPS)
N_TAIL = len(GROUPS) - N_PROJ
SLOTS_STEP = 8


def schedule(proj, tail):
    out, counts, at = [], {True: 0, False: 0}, 0
    for kind, n, pieces in GROUPS:
        of_proj = kind in PROJ
        if (proj if of_proj else tail):
            out.append((kind, n, at, pieces, len(out), counts[of_proj]))
            counts[of_proj] += 1
        at += pieces
    assert at <= STEPS * SLOTS_STEP
    return out


ALL = slice(None)


def both(pair, *index):
    return tuple(x[index] for x in pair)


def product(pe, out, w, x, start, stop):
    pe.matmul(out, w[0], x[0], start=start, stop=False)
    pe.matmul(out, w[0], x[1], start=False, stop=False)
    return pe.matmul(out, w[1], x[0], start=False, stop=stop)


def setup(nc, a, c, ps):
    with ExitStack() as ctx:
        sem = lambda n: ctx.enter_context(nc.semaphore(n))
        loaded = [sem(f"setup_loaded{i}") for i in range(5)]
        direct_loaded = sem("setup_direct_loaded")
        zeroed = sem("setup_zeroed")
        filled = sem("setup_filled")
        made = sem("setup_made")
        tables_written = sem("setup_tables_written")
        tr_done = sem("setup_tr_done")
        bank_free = [sem("setup_bank_free0"), sem("setup_bank_free1")]
        block = ctx.enter_context(nc.Block())
        raw_loaded = [sem(f"setup_raw_loaded{i}") for i in range(4)]
        hi_ready = sem("setup_hi_ready")
        raw = [c["qT0"], c["kT0"], c["v0"]]
        dst = [c["sgT"], c["suT"], c["sdT"]]
        rw_raw = c["xres0"][0:E, 0, :]
        bqk_raw = c["xres0"][0:2 * HG, 1, 0:P]
        plain = [c["qT1"], c["kT1"], c["v1"], c["x2n"]]
        split = [both(c["wqkv"], ALL, ALL, slice(n * D, (n + 1) * D)) for n in range(3)]
        split.append(both(c["wo"], ALL, ALL, ALL))
        jobs = [(w, k) for w in range(3) for k in range(DK)] + [(3, 0), (4, 0)]

        @block.sync
        def _(sp):
            for n in range(4):
                of = a["Wqkv"][:, n * D:(n + 1) * D] if n < 3 else a["Wo"]
                sp.dma_start(plain[n][:, :, :], of.rearrange("(k p) n -> p k n", p=P)).then_inc(raw_loaded[n], 16)
            for w, name in enumerate(("shared_gate", "shared_up", "shared_down")):
                sp.dma_start(raw[w][:, :, :], a[name].rearrange("(i p) d -> p i d", p=P)).then_inc(loaded[w], 16)
            sp.dma_start(rw_raw, a["router_w"]).then_inc(loaded[3], 16)
            sp.dma_start(bqk_raw, a["bqkv"][0:2 * D].rearrange("(f p) -> f p", p=P)).then_inc(loaded[4], 16)
            direct = [
                (c["bv"][:, :], a["bqkv"][2 * D:3 * D].rearrange("(o n) -> o n", o=1).broadcast_to([P, D])),
                (c["bo"][:, :], a["bo"].rearrange("(o n) -> o n", o=1).broadcast_to([P, D])),
                (c["ebias"][:, :], a["e_bias"].rearrange("(o n) -> o n", o=1).broadcast_to([P, E])),
            ]
            for to, of in direct:
                sp.dma_start(to, of).then_inc(direct_loaded, 16)
            sp.wait_ge(direct_loaded, 16 * len(direct))
            sp.wait_ge(filled, 2)
            sp.dma_start(a["slots"].rearrange("(e s) w -> e (s w)", e=E),
                         c["S"][0:E, 0:2, :].rearrange("e a n -> e (a n)")[:, 0:2 * CAPP]).then_inc(tables_written, 16)
            for name in ("x2n", "out"):
                for n in range(CS):
                    sp.dma_start(a[name][TOKENS + n * P:TOKENS + (n + 1) * P, :], c["S"][:, 2, :]).then_inc(tables_written, 16)
            sp.wait_ge(tables_written, 16 * (1 + 2 * CS))

        @block.gpsimd
        def _(pool):
            z = pool.memset(c["ident"][:, :], 0.0)
            pool.memset(c["maskrow"][:, :], 0.0)
            pool.memset(c["before"][:, :], 1.0)
            pool.memset(c["ones"][:, :], 1.0)
            pool.memset(c["half"][:, :], -0.5)
            pool.memset(c["carry"][:, :], 0.0)
            pool.memset(c["gval"][:, :, :], LOW)
            pool.memset(c["grep"][:, :, :], LOW)
            pool.memset(c["mval"][:, :, :], LOW)
            pool.memset(c["erep"][:, :, :], LOW)
            pool.memset(c["S"][:, :, :], 0.0).then_inc(zeroed, 1)
            pool.wait_ge(zeroed, 1)
            pool.affine_select(out=c["ident"][:, :], in_=c["ident"][:, :], compare_op=ALU.not_equal, fill=1.0,
                               base=0, pattern=[[-1, P]], channel_multiplier=1)
            tri = c["maskrow"][:, SEQ - P:SEQ]
            pool.affine_select(out=tri, in_=tri, compare_op=ALU.is_ge, fill=MASKED,
                               base=0, pattern=[[-1, P]], channel_multiplier=1)
            pool.affine_select(out=c["before"][:, :], in_=c["before"][:, :], compare_op=ALU.is_gt, fill=0.0,
                               base=0, pattern=[[1, P]], channel_multiplier=-1)
            pool.iota(c["tok_i"][:, :], pattern=[[P, TT]], base=0, channel_multiplier=1)
            pool.iota(c["eoff_i"][:, :, :], pattern=[[0, TT], [CAPP, E]], base=1, channel_multiplier=0)
            pool.iota(c["fill_i"], pattern=[[P, CS], [1, P]], base=TOKENS, channel_multiplier=0).then_inc(made, 1)

        def halves(w, k, bank):
            if w < 3:
                return both(dst[w], ALL, k, ALL), bank[:, :]
            return both(c["rwT"], ALL, ALL, ALL), bank[:, 0:DK * E].rearrange("p (k e) -> p k e", k=DK)

        @block.vector
        def _(dve):
            dve.wait_ge(made, 1)
            dve.tensor_copy(c["tok"][:, :], c["tok_i"][:, :])
            dve.tensor_copy(c["eoff"][:, :, :], c["eoff_i"][:, :, :]).then_inc(filled, 1)
            empty = c["S"][0:E, 0:2, :].rearrange("e a n -> e (a n)")[:, 0:2 * CAPP].rearrange("e (s w) -> e s w", w=2)
            dve.tensor_copy(empty[:, :, 0], c["fill_i"].rearrange("e c p -> e (c p)")).then_inc(filled, 1)
            for n in range(4):
                dve.wait_ge(hi_ready, n + 1)
                dve.scalar_tensor_tensor(split[n][1], plain[n][:, :, :], WS, split[n][0], ALU.mult, ALU.subtract)
            for n, (w, k) in enumerate(jobs):
                bank = ps["dense"][n % 2]
                if w < 4:
                    to, of = halves(w, k, bank)
                    dve.wait_ge(hi_ready, 4 + n + 1)
                    dve.scalar_tensor_tensor(to[1], of, WS, to[0], ALU.mult, ALU.subtract).then_inc(bank_free[n % 2], 1)
                else:
                    dve.wait_ge(tr_done, n + 1)
                    dve.tensor_copy(c["bqk"][:, :], bank[:, 0:2 * HG]).then_inc(bank_free[n % 2], 1)

        @block.scalar
        def _(act):
            for n in range(4):
                act.wait_ge(raw_loaded[n], 16)
                act.activation(split[n][0], plain[n][:, :, :], ACT.Copy, scale=WS).then_inc(hi_ready, 1)
            for n, (w, k) in enumerate(jobs):
                if w < 4:
                    act.wait_ge(tr_done, n + 1)
                    to, of = halves(w, k, ps["dense"][n % 2])
                    act.activation(to[0], of, ACT.Copy, scale=WS).then_inc(hi_ready, 1)

        @block.tensor
        def _(pe):
            pe.wait_ge(made, 1)
            for n, (w, k) in enumerate(jobs):
                if k == 0:
                    pe.wait_ge(loaded[w], 16)
                if n >= 2:
                    pe.wait_ge(bank_free[n % 2], n // 2)
                bank = ps["dense"][n % 2]
                for i in range(4 if w < 4 else 1):
                    if w == 4:
                        last = pe.transpose(bank[:, 0:2 * HG], bqk_raw, c["ident"][0:2 * HG, 0:2 * HG])
                    elif w < 3:
                        last = pe.transpose(bank[:, i * P:(i + 1) * P], raw[w][:, i, k * P:(k + 1) * P], c["ident"][:, :])
                    else:
                        last = pe.transpose(bank[:, i * E:(i + 1) * E], rw_raw[:, i * P:(i + 1) * P], c["ident"][0:E, 0:E])
                last.then_inc(tr_done, 1)


def sequences(nc, a, c, ps):
    with ExitStack() as ctx:
        sem = lambda n: ctx.enter_context(nc.semaphore(n))
        xin_loaded, xres_loaded = sem("xin_loaded"), sem("xres_loaded")
        x2n_stored, out_stored = sem("x2n_stored"), sem("out_stored")
        slots_scattered = sem("slots_scattered")
        proj_done, tail_done = sem("proj_done"), sem("tail_done")
        x1_ready, gate_used, pos_used = sem("x1_ready"), sem("gate_used"), sem("pos_used")
        xT_ready, qk_ready, v_ready, x2T_ready = sem("xT_ready"), sem("qk_ready"), sem("v_ready"), sem("x2T_ready")
        tanh_ready, glu_ready = sem("tanh_ready"), sem("glu_ready")
        xT_hi, x2T_hi, hT_hi, h_ready = sem("xT_hi"), sem("x2T_hi"), sem("hT_hi"), sem("h_ready")
        scores_done, masked_done, exp_done = sem("scores_done"), sem("masked_done"), sem("exp_done")
        pT_done, rden_ready = sem("pT_done"), sem("rden_ready")
        pT_copied = [sem("pT_copied_even"), sem("pT_copied_odd")]
        o_done, o_used = sem("o_done"), sem("o_used")
        ln1_stats, ln1_normed = sem("ln1_stats"), sem("ln1_normed")
        ln2_stats, ln2_normed = sem("ln2_stats"), sem("ln2_normed")
        rstd1_ready, rstd2_ready = sem("rstd1_ready"), sem("rstd2_ready")
        xres_biased, out_ready = sem("xres_biased"), sem("out_ready")
        sig_exp, sel_ready, dest_ready = sem("sig_exp"), sem("sel_ready"), sem("dest_ready")
        dve_chain, settled = sem("dve_chain"), sem("settled")
        block = ctx.enter_context(nc.Block())

        x_v = a["x"].rearrange("b (t p) d -> b p t d", p=P)
        x2n_v = a["x2n"][0:TOKENS, :].rearrange("(b t p) d -> b p t d", b=BATCH, p=P)
        out_v = a["out"][0:TOKENS, :].rearrange("(b t p) d -> b p t d", b=BATCH, p=P)

        def turns(eng, turn):
            turn(0, 0, True, False, False)
            turn(1, 1, True, True, False)
            with eng.Fori(0, (BATCH - 2) // 2) as pair:
                turn(pair * 2 + 2, 0, True, True, True)
                turn(pair * 2 + 3, 1, True, True, True)
            turn(BATCH, 0, False, True, True)
            turn(BATCH + 1, 1, False, False, True)

        def settle(eng):
            eng.sem_inc(settled, 1)

        def done_wait(eng, i, kind, at):
            if kind in PROJ:
                eng.wait_ge(proj_done, i * N_PROJ + at + 1)
            else:
                eng.wait_ge(tail_done, (i - 2) * N_TAIL + at + 1)

        def read_wait(eng, i, kind, m):
            b = i - 2
            if kind == "out":
                eng.wait_ge(x1_ready, b * TT + m + 1)
            elif kind == "xT":
                eng.wait_ge(xT_ready, i * TT + m + 1)
            elif kind in ("q", "k"):
                eng.wait_ge(qk_ready, i * 2 * HG + 2 * m + (kind == "k") + 1)
            elif kind == "v":
                eng.wait_ge(v_ready, i * TT + m + 1)
            elif kind == "x2T":
                eng.wait_ge(x2T_ready, b * TT + m + 1)
            elif kind == "router":
                eng.wait_ge(sig_exp, b + 1)
            elif kind == "gate":
                eng.wait_ge(gate_used, b * IB + m + 1)
            elif kind == "up":
                eng.wait_ge(glu_ready, b * IB + m + 1)
            elif kind == "pos":
                eng.wait_ge(pos_used, b + 1)
            elif kind == "down":
                eng.wait_ge(out_ready, (b + 1) * TT + m + 1)

        @block.sync
        def _(sp):
            def turn(i, par, proj, attn, fin):
                b = i - 2
                if attn:
                    if fin:
                        sp.wait_ge(xres_biased, (i - 1) * TT)
                        settle(sp)
                    sp.dma_start(c["xres"][1 - par][:, :, :], x_v[i - 1]).then_inc(xres_loaded, 16)
                if fin:
                    sp.wait_ge(ln2_normed, (b + 1) * TT)
                    sp.dma_start(x2n_v[b], c["x2n"][:, :, :]).then_inc(x2n_stored, 16)
                if proj:
                    sp.wait_ge(proj_done, i * N_PROJ + TT)
                    settle(sp)
                    if fin:
                        sp.wait_ge(x2T_ready, (b + 1) * TT)
                        settle(sp)
                        sp.wait_ge(x2n_stored, (b + 1) * 16)
                        settle(sp)
                    sp.dma_start(c["xin"][:, :, :], x_v[(i + 1) % BATCH]).then_inc(xin_loaded, 16)
                if fin:
                    sp.wait_ge(out_ready, (b + 2) * TT)
                    sp.dma_start(out_v[b], c["xres"][par][:, :, :]).then_inc(out_stored, 16)
                    sp.wait_ge(out_stored, (b + 1) * 16)
                    settle(sp)

            sp.dma_start(c["xin"][:, :, :], x_v[0]).then_inc(xin_loaded, 16)
            turns(sp, turn)
            sp.wait_ge(x2n_stored, 16 * BATCH)
            sp.wait_ge(out_stored, 16 * BATCH)

        @block.tensor
        def _(pe):
            ident = c["ident"][:, :]

            def dense(i, par, slot, groups, fin):
                hit = [g for g in groups if g[2] <= slot < g[2] + g[3]]
                if not hit:
                    return
                kind, m, first, pieces, pos, at = hit[0]
                k, b = slot - first, i - 2
                bank = ps["dense"][pos % DENSE]
                if k == 0 and pos >= DENSE:
                    read_wait(pe, i, *groups[pos - DENSE][0:2])
                elif k == 0 and not (isinstance(i, int) and i == 0):
                    pe.wait_ge(v_ready, min(i, BATCH) * TT if isinstance(i, int) else i * TT)
                    if fin:
                        pe.wait_ge(out_ready, (b + 1) * TT - (pos == 0))
                blk = slice(m * P, (m + 1) * P)
                if kind == "out":
                    if k == 0:
                        pe.wait_ge(o_used, b * STEPS + STEPS - TT + m + 1)
                    last = product(pe, bank[:, :], both(c["aT"], ALL, k, blk), both(c["wo"], ALL, k, ALL), k == 0, k == DK - 1)
                elif kind == "xT":
                    pe.wait_ge(ln1_normed, i * TT + m + 1)
                    for j in range(DK):
                        last = pe.transpose(bank[:, j * P:(j + 1) * P], c["xin"][:, m, j * P:(j + 1) * P], ident)
                elif kind in ("q", "k"):
                    if k == 0 and kind == "q" and m == 0:
                        pe.wait_ge(xT_ready, (i + 1) * TT)
                    off = (kind == "k") * D + m * P
                    last = product(pe, bank[:, :], both(c["wqkv"], ALL, k, slice(off, off + P)), both(c["xT"], ALL, k, ALL), k == 0, k == DK - 1)
                elif kind == "v":
                    last = product(pe, bank[:, :], both(c["xT"], ALL, k, blk), both(c["wqkv"], ALL, k, slice(2 * D, 3 * D)), k == 0, k == DK - 1)
                elif kind == "x2T":
                    pe.wait_ge(ln2_normed, b * TT + m + 1)
                    for j in range(DK):
                        last = pe.transpose(bank[:, j * P:(j + 1) * P], c["x2n"][:, m, j * P:(j + 1) * P], ident)
                elif kind == "router":
                    pe.wait_ge(x2T_ready, b * TT + k + 1)
                    for j in range(DK):
                        last = product(pe, bank[:, k * E:(k + 1) * E], both(c["xT"], ALL, j, slice(k * P, (k + 1) * P)),
                                       both(c["rwT"], ALL, j, ALL), j == 0, j == DK - 1)
                elif kind in ("gate", "up"):
                    w = c["sgT"] if kind == "gate" else c["suT"]
                    last = product(pe, bank[:, :], both(w, ALL, k, blk), both(c["xT"], ALL, k, ALL), k == 0, k == DK - 1)
                elif kind == "pos":
                    pe.wait_ge(sel_ready, b + 1)
                    sel = c["sel"][:, :, :].rearrange("p t e -> p (t e)")
                    n = TT * E
                    pe.matmul(bank[:, 0:n], c["ones"][:, :], c["carry4"][:, :, :].rearrange("p t e -> p (t e)"), start=True, stop=False)
                    pe.matmul(bank[:, 0:n], c["before"][:, :], sel, start=False, stop=False)
                    for s in range(1, TT):
                        last = pe.matmul(bank[:, s * E:n], c["ones"][:, :], sel[:, 0:n - s * E], start=False, stop=s == TT - 1)
                elif kind == "down":
                    if m == 0:
                        pe.wait_ge(h_ready, b * IB + k + 1)
                    last = product(pe, bank[:, :], both(c["hT"], ALL, k, blk), both(c["sdT"], ALL, k, ALL), k == 0, k == IB - 1)
                if k == pieces - 1:
                    last.then_inc(proj_done if kind in PROJ else tail_done, 1)

            def scores(i, par, s):
                hg, qt = divmod(s, TT)
                g = (i - 1) * STEPS + s
                if s == 0:
                    pe.wait_ge(qk_ready, i * 2 * HG)
                for h in range(GH):
                    if not (isinstance(i, int) and i == 1 and s == 0):
                        pe.wait_ge(pT_copied[h % 2], g * 2 - 1 + h // 2)
                    rows = slice(h * HD, (h + 1) * HD)
                    last = pe.matmul(ps["scores"][h][:, 0:(qt + 1) * P], c["qT"][par][rows, hg, qt * P:(qt + 1) * P],
                                     c["kT"][par][rows, hg, 0:(qt + 1) * P], start=True, stop=True)
                last.then_inc(scores_done, 1)

            def transpose_probs(i, s, h):
                g = (i - 1) * STEPS + s
                pe.wait_ge(exp_done, g * GH + h + 1)
                for kt in range(s % TT + 1):
                    last = pe.transpose(ps["scores"][h][:, kt * P:(kt + 1) * P], c["S"][:, h, kt * P:(kt + 1) * P], ident)
                last.then_inc(pT_done, 1)

            def values(i, par, s):
                hg, qt = divmod(s, TT)
                g = (i - 1) * STEPS + s
                if s == 0:
                    pe.wait_ge(v_ready, i * TT)
                for odd in range(2):
                    pe.wait_ge(pT_copied[odd], (g + 1) * (GH // 2))
                if not (isinstance(i, int) and i == 1 and s == 0):
                    pe.wait_ge(o_used, g)
                for kt in range(qt + 1):
                    for h in range(GH):
                        rows = slice(h * HD, (h + 1) * HD)
                        pe.matmul(ps["o"][rows, 0:P], c["v"][par][:, kt, hg * P + h * HD:hg * P + (h + 1) * HD],
                                  c["pT"][:, h, kt * P:(kt + 1) * P], start=kt == 0, stop=kt == qt)
                pe.wait_ge(rden_ready, g + 1)
                pe.transpose(ps["o"][:, P:2 * P], c["rden"][:, :, :].rearrange("p h d -> p (h d)"), ident).then_inc(o_done, 1)

            def turn(i, par, proj, attn, fin):
                groups = schedule(proj, fin)
                for s in range(STEPS):
                    slot = s * SLOTS_STEP
                    if attn:
                        scores(i, 1 - par, s)
                    dense(i, par, slot, groups, fin)
                    if s == 0 and fin:
                        values(i - 1, par, STEPS - 1)
                    if s > 0 and attn:
                        values(i, 1 - par, s - 1)
                    dense(i, par, slot + 1, groups, fin)
                    dense(i, par, slot + 2, groups, fin)
                    dense(i, par, slot + 3, groups, fin)
                    for h in range(GH):
                        if attn:
                            transpose_probs(i, s, h)
                        dense(i, par, slot + 4 + h, groups, fin)

            turns(pe, turn)

        @block.scalar
        def _(act):
            def copies(i, par, slot, groups):
                hit = [g for g in groups if g[2] + g[3] - 1 == slot]
                if not hit:
                    return
                kind, m, _, _, pos, at = hit[0]
                bank = ps["dense"][pos % DENSE]
                if kind in ("xT", "x2T"):
                    done_wait(act, i, kind, at)
                    act.activation(c["xT"][0][:, :, m * P:(m + 1) * P], bank[:, :].rearrange("p (k t) -> p k t", k=DK),
                                   ACT.Copy, scale=XS).then_inc(xT_hi if kind == "xT" else x2T_hi, 1)
                elif kind in ("q", "k"):
                    done_wait(act, i, kind, at)
                    f = (kind == "k") * HG + m
                    to = c["qT"] if kind == "q" else c["kT"]
                    act.activation(to[par][:, m, :], bank[:, :], ACT.Identity, bias=c["bqk"][:, f:f + 1],
                                   scale=1.0 / (XS * WS)).then_inc(qk_ready, 1)
                elif kind == "router":
                    done_wait(act, i, kind, at)
                    act.activation(c["sig"][:, :, :].rearrange("p t e -> p (t e)"), bank[:, 0:TT * E], ACT.Exp,
                                   scale=-1.0 / (XS * WS)).then_inc(sig_exp, 1)
                elif kind == "gate":
                    done_wait(act, i, kind, at)
                    if m >= 2:
                        act.wait_ge(h_ready, (i - 2) * IB + m - 1)
                    act.activation(c["glu"][:, m % 2, :], bank[:, :], ACT.Tanh, scale=0.5 / (XS * WS)).then_inc(tanh_ready, 1)
                if kind == "up" and m > 0:
                    h_hi(i, m - 1)

            def norm(x, to, mv, rstd, count, done):
                act.wait_ge(rstd, count * 3)
                act.activation(to, x, ACT.Identity, bias=mv[:, 0:1], scale=mv[:, 1:2]).then_inc(done, 1)

            def norms(i, par, slot, proj, fin):
                if proj and slot in LN1_SLOT:
                    norm1(i + 1, LN1_SLOT[slot])
                if fin and slot in LN2_SLOT:
                    t, b = LN2_SLOT[slot], i - 2
                    if isinstance(i, int) and i == BATCH and t == 0:
                        act.wait_ge(ln1_normed, (BATCH + 1) * TT)
                    norm(c["xres"][par][:, t, :], c["x2n"][:, t, :], c["mv2"][:, t, :], rstd2_ready, b * TT + t + 1, ln2_normed)
                if fin and slot == LAST_H:
                    h_hi(i, IB - 1)

            def norm1(j, t):
                norm(c["xin"][:, t, :], c["xin"][:, t, :], c["mv1"][:, t, :], rstd1_ready, j * TT + t + 1, ln1_normed)

            def h_hi(i, m):
                act.wait_ge(glu_ready, (i - 2) * IB + m + 1)
                act.activation(c["hT"][0][:, m, :], c["glu"][:, m % 2, :], ACT.Copy, scale=HS / (XS * WS) ** 2).then_inc(hT_hi, 1)

            def exp(i, s, h):
                g = (i - 1) * STEPS + s
                row = c["S"][:, h, 0:(s % TT + 1) * P]
                act.wait_ge(masked_done, g * GH + h + 1)
                act.activation(row, row, ACT.Exp, bias=c["nmax"][:, h:h + 1], scale=-1.0,
                               accum_out=c["den"][:, h:h + 1]).then_inc(exp_done, 1)

            def copy_probs(i, s, h):
                g = (i - 1) * STEPS + s
                n = (s % TT + 1) * P
                act.wait_ge(pT_done, g * GH + h + 1)
                act.activation(c["pT"][:, h, 0:n], ps["scores"][h][:, 0:n], ACT.Copy).then_inc(pT_copied[0], 1)

            def turn(i, par, proj, attn, fin):
                groups = schedule(proj, fin)
                for s in range(STEPS):
                    slot = s * SLOTS_STEP
                    if attn:
                        exp(i, s, 0)
                        exp(i, s, 1)
                    copies(i, par, slot, groups)
                    norms(i, par, slot, proj, fin)
                    if attn:
                        exp(i, s, 2)
                        exp(i, s, 3)
                    copies(i, par, slot + 1, groups)
                    norms(i, par, slot + 1, proj, fin)
                    copies(i, par, slot + 2, groups)
                    norms(i, par, slot + 2, proj, fin)
                    copies(i, par, slot + 3, groups)
                    norms(i, par, slot + 3, proj, fin)
                    if attn:
                        copy_probs(i, s, 0)
                    for n in (4, 5):
                        copies(i, par, slot + n, groups)
                        norms(i, par, slot + n, proj, fin)
                    if attn:
                        copy_probs(i, s, 2)
                    for n in (6, 7):
                        copies(i, par, slot + n, groups)
                        norms(i, par, slot + n, proj, fin)

            for t in range(TT):
                norm1(0, t)
            turns(act, turn)

        @block.vector
        def _(dve):
            chain = {"turn": 0, "links": 0}

            def link(ins):
                chain["links"] += 1
                ins.then_inc(dve_chain, 1)
                dve.wait_ge(dve_chain, chain["turn"] + chain["links"])

            def statistics(x, stats, mv):
                link(dve.bn_stats(stats, x))
                settle(dve)
                return dve.bn_aggr(mv, stats)

            flat = lambda t: t[:, :, :].rearrange("p t e -> p (t e)")

            def route_scores(i):
                dve.wait_ge(sig_exp, i - 1)
                link(dve.tensor_scalar_add(flat(c["sig"]), flat(c["sig"]), 1.0))
                link(dve.reciprocal(flat(c["sig"]), flat(c["sig"])))
                link(dve.tensor_tensor(c["sc"][:, :, :], c["sig"][:, :, :], c["ebias"][:, :].unsqueeze(1).broadcast_to([P, TT, E]), ALU.add))
                s4 = flat(c["sc"]).rearrange("p (g e) -> p g e", e=GE)
                hi, lo, m1, m2 = c["hi"][:, :, :], c["lo"][:, :, :], c["m1"][:, :], c["m2"][:, :]
                dve.tensor_tensor(hi, s4[:, :, 0:2], s4[:, :, 2:4], ALU.max)
                link(dve.tensor_tensor(lo, s4[:, :, 0:2], s4[:, :, 2:4], ALU.min))
                dve.tensor_tensor(m1, hi[:, :, 0], hi[:, :, 1], ALU.max)
                dve.tensor_tensor(m2, hi[:, :, 0], hi[:, :, 1], ALU.min)
                link(dve.tensor_tensor(lo[:, :, 0], lo[:, :, 0], lo[:, :, 1], ALU.max))
                link(dve.tensor_tensor(m2, m2, lo[:, :, 0], ALU.max))
                group = lambda t: t.rearrange("p (t g) -> p t g", t=TT)
                link(dve.tensor_tensor(c["gval"][:, :, 0:NG], group(m1), group(m2), ALU.add))

            def route_groups(i):
                settle(dve)
                for t in range(TT):
                    last = dve.max(c["top8"][:, t, :], c["gval"][:, t, 0:NG])
                link(last)
                link(dve.tensor_copy(c["grep"][:, :, 0:TOPG], c["top8"][:, :, 0:TOPG]))
                settle(dve)
                for t in range(TT):
                    last = dve.match_replace(c["gout"][:, t, :], c["grep"][:, t, :], c["gval"][:, t, :], HIGH)
                link(last)
                link(dve.tensor_scalar(c["gmask"][:, :, :], c["gout"][:, :, 0:NG], HIGH / 2, None, ALU.is_ge))

            def route_mask(i):
                for t in range(TT):
                    last = dve.tensor_tensor(c["mval"][:, t, 0:E].rearrange("p (g e) -> p g e", e=GE),
                                             c["sc"][:, t, :].rearrange("p (g e) -> p g e", e=GE),
                                             c["gmask"][:, t, :].unsqueeze(2).broadcast_to([P, NG, GE]), ALU.mult)
                link(last)
                link(dve.tensor_scalar_add(c["mval"][:, :, 0:E], c["mval"][:, :, 0:E], 0.0))

            def route_best(i):
                settle(dve)
                for t in range(TT):
                    last = dve.max(c["top8"][:, t, :], c["mval"][:, t, 0:E])
                link(last)
                link(dve.tensor_copy(c["erep"][:, :, 0:TOPK], c["top8"][:, :, 0:TOPK]))

            def route_select(i):
                settle(dve)
                for t in range(TT):
                    last = dve.match_replace(c["eout"][:, t, :], c["erep"][:, t, :], c["mval"][:, t, :], HIGH)
                link(last)
                link(dve.tensor_scalar(c["sel"][:, :, :], c["eout"][:, :, 0:E], HIGH / 2, None, ALU.is_ge))
                dve.tensor_copy(c["carry4"][:, :, :], c["carry"][:, :].unsqueeze(1).broadcast_to([P, TT, E])).then_inc(sel_ready, 1)

            def route_weights(i):
                link(dve.tensor_tensor(flat(c["wgt"]), flat(c["sig"]), flat(c["sel"]), ALU.mult))
                dve.tensor_reduce(c["count"][:, :], c["sel"][:, :, :].rearrange("p t e -> p e t"), AX.X, ALU.add)
                link(dve.tensor_reduce(c["wsum"][:, :], c["wgt"][:, :, :], AX.X, ALU.add))
                dve.tensor_tensor(c["carry"][:, :], c["carry"][:, :], c["count"][:, :], ALU.add)
                link(dve.tensor_scalar_add(c["wsum"][:, :], c["wsum"][:, :], 1e-20))
                link(dve.reciprocal(c["wsum"][:, :], c["wsum"][:, :]))
                link(dve.tensor_scalar_mul(c["wsum"][:, :], c["wsum"][:, :], ROUTE_SCALE / 2 / (HS * WS)))
                link(dve.tensor_tensor(c["wgt"][:, :, :], c["wgt"][:, :, :], c["wsum"][:, :].unsqueeze(2).broadcast_to([P, TT, E]), ALU.mult))

            ROUTE = (route_scores, route_groups, route_mask, route_best, route_select, route_weights)

            def dest_keys(i, bank):
                n = TT * E
                dve.scalar_tensor_tensor(flat(c["eout"])[:, 0:n], bank[:, 0:n], float(CAP), flat(c["sel"]), ALU.is_lt, ALU.mult)
                dve.tensor_tensor(flat(c["sc"]), bank[:, 0:n], flat(c["eoff"]), ALU.add).then_inc(pos_used, 1)
                dve.wait_ge(pos_used, i - 1)
                link(dve.tensor_tensor(flat(c["sc"]), flat(c["sc"]), flat(c["eout"])[:, 0:n], ALU.mult))

            def dest_slots(i, bank):
                settle(dve)
                for t in range(TT):
                    last = dve.max(c["top8"][:, t, :], c["sc"][:, t, :])
                link(last)
                for t in range(TT):
                    last = dve.tensor_tensor(c["eq"][:, t, :, :], c["sc"][:, t, :].unsqueeze(1).broadcast_to([P, TOPK, E]),
                                             c["top8"][:, t, 0:TOPK].unsqueeze(2).broadcast_to([P, TOPK, E]), ALU.is_equal)
                link(last)

            def dest_weights(i, bank):
                for t in range(TT):
                    last = dve.tensor_tensor(c["eq"][:, t, :, :], c["eq"][:, t, :, :],
                                             c["wgt"][:, t, :].unsqueeze(1).broadcast_to([P, TOPK, E]), ALU.mult)
                link(last)
                dve.tensor_reduce(c["rec"][:, :, :, 1], c["eq"][:, :, :, :], AX.X, ALU.add)
                dve.tensor_copy(c["rec"][:, :, :, 0], c["tok"][:, :].unsqueeze(2).broadcast_to([P, TT, TOPK]))

            def dest_records(i, bank):
                top = c["top8"][:, :, 0:TOPK]
                link(dve.tensor_scalar(c["none"][:, :, :], top, 0.5, float(1 << 20), ALU.is_lt, ALU.mult))
                link(dve.scalar_tensor_tensor(c["idxf"][:, :, :], top, -1.0, c["none"][:, :, :], ALU.add, ALU.add))
                link(dve.tensor_copy(c["idx"][:, :, :], c["idxf"][:, :, :]))
                dve.tensor_scalar_add(c["tok"][:, :], c["tok"][:, :], float(SEQ)).then_inc(dest_ready, 1)

            DESTINATIONS = (dest_keys, dest_slots, dest_weights, dest_records)

            def statistics1(j, t):
                if t == 0:
                    dve.wait_ge(xin_loaded, (j + 1) * 16)
                statistics(c["xin"][:, t, :], c["stats1"][:, t, :], c["mv1"][:, t, :]).then_inc(ln1_stats, 1)

            def between(i, slot, groups, proj, fin):
                if fin and slot in ROUTE_SLOT:
                    ROUTE[ROUTE_SLOT[slot]](i)
                if fin and slot in DEST_SLOT:
                    bank, at = [(ps["dense"][g[4] % DENSE], g[5]) for g in groups if g[0] == "pos"][0]
                    if DEST_SLOT[slot] == 0:
                        done_wait(dve, i, "pos", at)
                    DESTINATIONS[DEST_SLOT[slot]](i, bank)
                if fin and slot == LAST_H:
                    h_lo(i, IB - 1)
                if proj and slot in STAT_SLOT:
                    statistics1(i + 1, STAT_SLOT[slot])

            def copies(i, par, slot, groups):
                hit = [g for g in groups if g[2] + g[3] - 1 == slot]
                if not hit:
                    return
                kind, m, _, _, pos, at = hit[0]
                bank, b = ps["dense"][pos % DENSE], i - 2
                if kind == "out":
                    x1 = c["xres"][par][:, m, :]
                    dve.wait_ge(xres_biased, (b + 1) * TT)
                    done_wait(dve, i, kind, at)
                    dve.scalar_tensor_tensor(x1, bank[:, :], 1.0 / (AS * WS), x1, ALU.mult, ALU.add).then_inc(x1_ready, 1)
                    dve.wait_ge(x1_ready, b * TT + m + 1)
                    statistics(x1, c["stats2"][:, m, :], c["mv2"][:, m, :]).then_inc(ln2_stats, 1)
                elif kind == "v":
                    done_wait(dve, i, kind, at)
                    dve.scalar_tensor_tensor(c["v"][par][:, m, :], bank[:, :], 1.0 / (XS * WS), c["bv"][:, :],
                                             ALU.mult, ALU.add).then_inc(v_ready, 1)
                elif kind in ("xT", "x2T"):
                    n = (i * TT + m + 1) if kind == "xT" else (b * TT + m + 1)
                    dve.wait_ge(xT_hi if kind == "xT" else x2T_hi, n)
                    cols = slice(m * P, (m + 1) * P)
                    dve.scalar_tensor_tensor(c["xT"][1][:, :, cols], bank[:, :].rearrange("p (k t) -> p k t", k=DK), XS,
                                             c["xT"][0][:, :, cols], ALU.mult, ALU.subtract
                                             ).then_inc(xT_ready if kind == "xT" else x2T_ready, 1)
                elif kind == "gate":
                    dve.wait_ge(tanh_ready, b * IB + m + 1)
                    glu = c["glu"][:, m % 2, :]
                    dve.scalar_tensor_tensor(glu, glu, 1.0, bank[:, :], ALU.add, ALU.mult).then_inc(gate_used, 1)
                elif kind == "up":
                    done_wait(dve, i, kind, at)
                    dve.wait_ge(gate_used, b * IB + m + 1)
                    glu = c["glu"][:, m % 2, :]
                    dve.tensor_tensor(glu, glu, bank[:, :], ALU.mult).then_inc(glu_ready, 1)
                    if m > 0:
                        h_lo(i, m - 1)
                elif kind == "down":
                    done_wait(dve, i, kind, at)
                    x1 = c["xres"][par][:, m, :]
                    dve.scalar_tensor_tensor(x1, bank[:, :], 0.5 / (HS * WS), x1, ALU.mult, ALU.add).then_inc(out_ready, 1)

            def h_lo(i, m):
                dve.wait_ge(hT_hi, (i - 2) * IB + m + 1)
                dve.scalar_tensor_tensor(c["hT"][1][:, m, :], c["glu"][:, m % 2, :], HS / (XS * WS) ** 2, c["hT"][0][:, m, :],
                                         ALU.mult, ALU.subtract).then_inc(h_ready, 1)

            def mask(i, s, h):
                g = (i - 1) * STEPS + s
                n = (s % TT + 1) * P
                if h == 0:
                    dve.wait_ge(scores_done, g + 1)
                settle(dve)
                dve.tensor_tensor_reduce(out=c["S"][:, h, 0:n], in0=ps["scores"][h][:, 0:n], in1=c["maskrow"][:, SEQ - n:SEQ],
                                         scale=-SCALE, scalar=HIGH, op0=ALU.add, op1=ALU.min,
                                         accum_out=c["nmax"][:, h:h + 1]).then_inc(masked_done, 1)

            def copy_probs(i, s, h):
                g = (i - 1) * STEPS + s
                n = (s % TT + 1) * P
                dve.wait_ge(pT_done, g * GH + h + 1)
                dve.tensor_copy(c["pT"][:, h, 0:n], ps["scores"][h][:, 0:n]).then_inc(pT_copied[1], 1)

            def denominators(i, s):
                g = (i - 1) * STEPS + s
                dve.wait_ge(exp_done, (g + 1) * GH)
                if not (isinstance(i, int) and i == 1 and s == 0):
                    dve.wait_ge(o_done, g)
                link(dve.reciprocal(c["den"][:, :], c["den"][:, :]))
                dve.tensor_copy(c["rden"][:, :, :], c["den"][:, :].unsqueeze(2).broadcast_to([P, GH, HD])).then_inc(rden_ready, 1)

            def normalise(i, s):
                hg, qt = divmod(s, TT)
                g = (i - 1) * STEPS + s
                dve.wait_ge(o_done, g + 1)
                cols = slice(qt * P, (qt + 1) * P)
                hi, lo = both(c["aT"], ALL, hg, cols)
                link(dve.tensor_copy(c["rdenT"][:, :], ps["o"][:, P:2 * P]))
                link(dve.scalar_tensor_tensor(c["att"][:, :], ps["o"][:, 0:P], AS, c["rdenT"][:, :], ALU.mult, ALU.mult))
                link(dve.tensor_copy(hi, c["att"][:, :]))
                dve.tensor_tensor(lo, c["att"][:, :], hi, ALU.subtract).then_inc(o_used, 1)

            def turn(i, par, proj, attn, fin):
                groups = schedule(proj, fin)
                chain["links"] = 0

                def place(slot):
                    copies(i, par, slot, groups)
                    between(i, slot, groups, proj, fin)

                for s in range(STEPS):
                    slot = s * SLOTS_STEP
                    if attn:
                        for h in range(GH):
                            mask(i, s, h)
                    place(slot)
                    if s == 0 and fin:
                        normalise(i - 1, STEPS - 1)
                    if s > 0 and attn:
                        normalise(i, s - 1)
                    for n in (1, 2, 3, 4):
                        place(slot + n)
                    if attn:
                        copy_probs(i, s, 1)
                    for n in (5, 6):
                        place(slot + n)
                    if attn:
                        copy_probs(i, s, 3)
                        denominators(i, s)
                    place(slot + 7)
                chain["turn"] += chain["links"]

            def counted(i, par, proj, attn, fin):
                if isinstance(i, int):
                    turn(i, par, proj, attn, fin)
                else:
                    start = chain.setdefault("loop", chain["turn"])
                    chain["turn"] = (i - 2) * LINKS + start
                    turn(i, par, proj, attn, fin)
                    assert chain["links"] == LINKS, chain["links"]
                    chain["turn"] = start + (BATCH - 2) * LINKS

            dve.sem_inc(out_ready, TT)
            for t in range(TT):
                statistics1(0, t)
            chain["turn"] = chain["links"]
            turns(dve, counted)

        @block.gpsimd
        def _(pool):
            def scales(mv, rstd, count):
                settle(pool)
                pool.tensor_scalar(mv[:, 1:2], mv[:, 1:2], EPS, None, ALU.add).then_inc(rstd, 1)
                pool.wait_ge(rstd, count * 3 - 2)
                pool.tensor_tensor(mv[:, 1:2], mv[:, 1:2], c["half"][:, :], ALU.pow).then_inc(rstd, 1)
                pool.wait_ge(rstd, count * 3 - 1)
                settle(pool)
                pool.tensor_scalar(mv[:, 0:1], mv[:, 0:1], mv[:, 1:2], -1.0, ALU.mult, ALU.mult).then_inc(rstd, 1)

            def scales1(j):
                for t in range(TT):
                    pool.wait_ge(ln1_stats, j * TT + t + 1)
                    scales(c["mv1"][:, t, :], rstd1_ready, j * TT + t + 1)

            def turn(i, par, proj, attn, fin):
                b = i - 2
                for t in range(TT):
                    if fin:
                        pool.wait_ge(ln2_stats, b * TT + t + 1)
                        scales(c["mv2"][:, t, :], rstd2_ready, b * TT + t + 1)
                if attn:
                    pool.wait_ge(xres_loaded, (i) * 16)
                    for t in range(TT):
                        xt = c["xres"][1 - par][:, t, :]
                        pool.tensor_tensor(xt, xt, c["bo"][:, :], ALU.add).then_inc(xres_biased, 1)
                if proj:
                    scales1(i + 1)
                if fin:
                    pool.wait_ge(dest_ready, b + 1)
                    settle(pool)
                    for t in range(TT):
                        for k in range(TOPK):
                            pool.indirect_dma_start(
                                out=a["slots"], out_offset=bass.IndirectOffsetOnAxis(ap=c["idx"][:, t, k:k + 1], axis=0),
                                in_=c["rec"][:, t, k, :], in_offset=None, bounds_check=SLOTS - 1,
                                oob_is_err=False).then_inc(slots_scattered, 16)
                    pool.wait_ge(x2n_stored, (b + 1) * 16)
                    settle(pool)
                    pool.wait_ge(slots_scattered, (b + 1) * (TT * TOPK * 16))
                    settle(pool)

            scales1(0)
            turns(pool, turn)


def experts(nc, a, e_, ps):
    with ExitStack() as ctx:
        sem = lambda n: ctx.enter_context(nc.semaphore(n))
        table_loaded, table_split, table_T, table_ready = sem("table_loaded"), sem("table_split"), sem("table_T"), sem("table_ready")
        gidx_ready, sidx_ready, wcol_ready = sem("gidx_ready"), sem("sidx_ready"), sem("wcol_ready")
        gathered = [sem("gathered0"), sem("gathered1")]
        w_loaded = [sem("w_loaded0"), sem("w_loaded1")]
        w_hi, w_ready = sem("w_hi"), sem("w_ready")
        xT_done, xT_hi, xT_copied = sem("ex_xT_done"), sem("ex_xT_hi"), sem("ex_xT_copied")
        gu_done, tanh_ready, glu_ready = sem("ex_gu_done"), sem("ex_tanh_ready"), sem("ex_glu_ready")
        h_hi, h_ready = sem("ex_h_hi"), sem("ex_h_ready")
        y_done, y_ready, y_added = sem("y_done"), sem("y_ready"), sem("y_added")
        settled = sem("ex_settled")
        block = ctx.enter_context(nc.Block())

        def settle(eng):
            eng.sem_inc(settled, 1)

        rows = lambda ch: P if ch < CS - 1 else LASTC
        WEIGHTS = (("wg", "W_gate"), ("wu", "W_up"), ("wd", "W_down"))
        arrived = lambda e, q, n: (e + 2 - q) * (n * 8)

        def experts_of(eng, expert):
            expert(0, 0, 2)
            expert(1, 1, 2)
            with eng.Fori(1, E // 2 - 1) as pair:
                expert(pair * 2, 0, 2)
                expert(pair * 2 + 1, 1, 2)
            expert(E - 2, 0, 1)
            expert(E - 1, 1, 0)

        is_first = lambda e, n: isinstance(e, int) and e < n

        @block.sync
        def _(sp):
            sp.dma_start(e_["table"][:, :], a["slots"].rearrange("(r s) w -> r (s w)", s=P)).then_inc(table_loaded, 16)

            def load(e, q):
                for name, of in WEIGHTS:
                    sp.dma_start(e_["raw_" + name][q][:, :, :], a[of].rearrange("e (k p) n -> e p k n", p=P)[e]).then_inc(w_loaded[q], 16)

            load(0, 0)
            load(1, 1)

            def expert(e, q, more):
                if more == 2:
                    sp.wait_ge(w_ready, (e + 1) * 3)
                    settle(sp)
                    load(e + 2, q)

            experts_of(sp, expert)

        @block.gpsimd
        def _(pool):
            pool.wait_ge(table_ready, 2)

            def gather(e, q):
                pool.tensor_copy(e_["gidx"][q][:, :], e_["tok"][:, bass.ds(e * CS, CS)]).then_inc(gidx_ready, 1)
                pool.wait_ge(gidx_ready, e + 1)
                settle(pool)
                for ch in range(CS):
                    r = rows(ch)
                    pool.indirect_dma_start(
                        out=e_["xg"][q][0:r, ch, :], out_offset=None, in_=a["x2n"],
                        in_offset=bass.IndirectOffsetOnAxis(ap=e_["gidx"][q][0:r, ch:ch + 1], axis=0)).then_inc(gathered[q], 16)

            gather(0, 0)
            gather(1, 1)

            def expert(e, q, more):
                if more == 2:
                    pool.wait_ge(xT_done, (e + 1) * CS)
                    settle(pool)
                    gather(e + 2, q)
                pool.tensor_copy(e_["sidx"][q][:, :], e_["tok"][:, bass.ds(e * CS, CS)]).then_inc(sidx_ready, 1)
                pool.wait_ge(sidx_ready, e + 1)
                settle(pool)
                pool.wait_ge(y_ready, (e + 1) * CS)
                settle(pool)
                if not is_first(e, 1):
                    pool.wait_ge(y_added, e * CS * 16)
                    settle(pool)
                for ch in range(CS):
                    r = rows(ch)
                    pool.indirect_dma_start(
                        out=a["out"], out_offset=bass.IndirectOffsetOnAxis(ap=e_["sidx"][q][0:r, ch:ch + 1], axis=0),
                        in_=e_["y"][q][0:r, ch, :], in_offset=None, compute_op=ALU.add).then_inc(y_added, 16)

            experts_of(pool, expert)
            pool.wait_ge(y_added, E * CS * 16)

        @block.tensor
        def _(pe):
            pe.wait_ge(table_split, 2)
            nr = E * CS
            for w in range(2):
                pe.transpose(ps["scores"][w][:, 0:nr], e_["split"][:, w, :], e_["ident"][0:nr, 0:nr]).then_inc(table_T, 1)

            def transposes(e, q):
                pe.wait_ge(gathered[q], arrived(e, q, CS))
                for ch in range(CS):
                    r, m = rows(ch), e * CS + ch
                    if not (isinstance(e, int) and m < 2):
                        pe.wait_ge(xT_copied, m - 1)
                    settle(pe)
                    bank = [ps["dense"][2], ps["o"]][(q * CS + ch) % 2]
                    for k in range(DK):
                        last = pe.transpose(bank[:, k * P:k * P + r], e_["xg"][q][0:r, ch, k * P:(k + 1) * P], e_["ident"][0:r, 0:r])
                    last.then_inc(xT_done, 1)

            transposes(0, 0)

            def expert(e, q, more):
                pe.wait_ge(w_ready, (e + 1) * 3)
                pe.wait_ge(xT_copied, (e + 1) * CS)
                if not is_first(e, 1):
                    pe.wait_ge(glu_ready, e * 2 * JB)
                for j in range(JB):
                    for n, w in enumerate(("wg", "wu")):
                        for k in range(DK):
                            last = product(pe, ps["scores"][2 * j + n][:, 0:CAP], both(e_[w][q], ALL, k, slice(j * P, (j + 1) * P)),
                                           both(e_["xT"], ALL, k, ALL), k == 0, k == DK - 1)
                        last.then_inc(gu_done, 1)
                if more:
                    transposes(e + 1, 1 - q)
                for ch in range(CS):
                    r, m = rows(ch), e * CS + ch
                    if not (isinstance(e, int) and m < 2):
                        pe.wait_ge(y_ready, m - 1)
                    for j in range(JB):
                        if ch == 0:
                            pe.wait_ge(h_ready, e * JB + j + 1)
                        last = product(pe, ps["dense"][(q * CS + ch) % 2][0:r, :], both(e_["hT"], ALL, j, slice(ch * P, ch * P + r)),
                                       both(e_["wd"][q], ALL, j, ALL), j == 0, j == JB - 1)
                    last.then_inc(y_done, 1)

            experts_of(pe, expert)

        @block.scalar
        def _(act):
            def weights_hi(e, q):
                act.wait_ge(w_loaded[q], arrived(e, q, 3))
                if not is_first(e, 2):
                    act.wait_ge(y_done, (e - 1) * CS)
                for name, _ in WEIGHTS:
                    act.activation(e_[name][q][0][:, :, :], e_["raw_" + name][q][:, :, :], ACT.Copy, scale=WS).then_inc(w_hi, 1)

            def copies(e, q):
                for ch in range(CS):
                    r, m = rows(ch), e * CS + ch
                    act.wait_ge(xT_done, m + 1)
                    bank = [ps["dense"][2], ps["o"]][(q * CS + ch) % 2]
                    act.activation(e_["xT"][0][:, :, ch * P:ch * P + r], bank[:, :].rearrange("p (k t) -> p k t", k=DK)[:, :, 0:r],
                                   ACT.Copy, scale=XS).then_inc(xT_hi, 1)

            weights_hi(0, 0)
            copies(0, 0)
            weights_hi(1, 1)

            def expert(e, q, more):
                for j in range(JB):
                    act.wait_ge(gu_done, e * 2 * JB + 2 * j + 1)
                    act.activation(e_["glu"][:, j, :], ps["scores"][2 * j][:, 0:CAP], ACT.Tanh, scale=0.5 / (XS * WS)).then_inc(tanh_ready, 1)
                for j in range(JB):
                    act.wait_ge(glu_ready, e * 2 * JB + 2 * j + 2)
                    act.activation(e_["hT"][0][:, j, :], e_["glu"][:, j, :], ACT.Copy, scale=HS / (XS * WS) ** 2).then_inc(h_hi, 1)
                if more:
                    copies(e + 1, 1 - q)
                if not is_first(e, 2):
                    act.wait_ge(y_added, (e - 1) * CS * 16)
                act.wait_ge(wcol_ready, e + 1)
                for ch in range(CS):
                    r, m = rows(ch), e * CS + ch
                    act.wait_ge(y_done, m + 1)
                    act.activation(e_["y"][q][0:r, ch, :], ps["dense"][(q * CS + ch) % 2][0:r, :], ACT.Copy,
                                   scale=e_["wcol"][q][0:r, ch:ch + 1]).then_inc(y_ready, 1)
                if more == 2:
                    weights_hi(e + 2, q)

            experts_of(act, expert)

        @block.vector
        def _(dve):
            dve.wait_ge(table_loaded, 16)
            pairs_v = e_["table"][:, :].rearrange("r (s w) -> r s w", w=2)
            for w in range(2):
                dve.tensor_copy(e_["split"][:, w, :], pairs_v[:, :, w]).then_inc(table_split, 1)
            dve.wait_ge(table_T, 2)
            dve.tensor_copy(e_["tok"][:, :], ps["scores"][0][:, 0:E * CS]).then_inc(table_ready, 1)
            dve.tensor_copy(e_["w"][:, :], ps["scores"][1][:, 0:E * CS]).then_inc(table_ready, 1)
            dve.wait_ge(table_ready, 2)

            def weights_lo(e, q):
                for n, (name, _) in enumerate(WEIGHTS):
                    dve.wait_ge(w_hi, e * 3 + n + 1)
                    dve.scalar_tensor_tensor(e_[name][q][1][:, :, :], e_["raw_" + name][q][:, :, :], WS, e_[name][q][0][:, :, :],
                                             ALU.mult, ALU.subtract).then_inc(w_ready, 1)

            def copies(e, q):
                for ch in range(CS):
                    r, m = rows(ch), e * CS + ch
                    dve.wait_ge(xT_hi, m + 1)
                    bank, cols = [ps["dense"][2], ps["o"]][(q * CS + ch) % 2], slice(ch * P, ch * P + r)
                    dve.scalar_tensor_tensor(e_["xT"][1][:, :, cols], bank[:, :].rearrange("p (k t) -> p k t", k=DK)[:, :, 0:r], XS,
                                             e_["xT"][0][:, :, cols], ALU.mult, ALU.subtract).then_inc(xT_copied, 1)

            weights_lo(0, 0)
            copies(0, 0)
            weights_lo(1, 1)

            def expert(e, q, more):
                dve.tensor_copy(e_["wcol"][q][:, :], e_["w"][:, bass.ds(e * CS, CS)]).then_inc(wcol_ready, 1)
                for j in range(JB):
                    glu = e_["glu"][:, j, :]
                    dve.wait_ge(tanh_ready, e * JB + j + 1)
                    dve.scalar_tensor_tensor(glu, glu, 1.0, ps["scores"][2 * j][:, 0:CAP], ALU.add, ALU.mult).then_inc(glu_ready, 1)
                    dve.wait_ge(gu_done, e * 2 * JB + 2 * j + 2)
                    dve.wait_ge(glu_ready, e * 2 * JB + 2 * j + 1)
                    dve.tensor_tensor(glu, glu, ps["scores"][2 * j + 1][:, 0:CAP], ALU.mult).then_inc(glu_ready, 1)
                for j in range(JB):
                    dve.wait_ge(h_hi, e * JB + j + 1)
                    dve.scalar_tensor_tensor(e_["hT"][1][:, j, :], e_["glu"][:, j, :], HS / (XS * WS) ** 2, e_["hT"][0][:, j, :],
                                             ALU.mult, ALU.subtract).then_inc(h_ready, 1)
                if more:
                    copies(e + 1, 1 - q)
                if more == 2:
                    weights_lo(e + 2, q)

            experts_of(dve, expert)


LINKS = 102


def transformer_block(nc, a):
    with ExitStack() as ctx:
        def pb(name):
            return ctx.enter_context(nc.psum_tensor(name, [P, 512], F32))

        ps = {"scores": [pb(f"scores{g}") for g in range(GH)], "o": pb("o_ps"),
              "dense": [pb(f"dense{n}") for n in range(DENSE)]}
        ident = ctx.enter_context(nc.sbuf_tensor("ident", [P, P], F32))
        with ExitStack() as first:
            def sb(name, shape, dt=F32):
                return first.enter_context(nc.sbuf_tensor(name, shape, dt))

            c = {"ident": ident}
            def pair(name, shape):
                return sb(name + "_hi", shape, F16), sb(name + "_lo", shape, F16)

            c["wqkv"] = pair("wqkv", [P, DK, 3 * D])
            c["rwT"] = pair("rwT", [P, DK, E])
            for n in ("wo", "sgT", "suT", "sdT", "xT", "aT", "hT"):
                c[n] = pair(n, [P, 4, 512])
            for n in ("qT0", "qT1", "kT0", "kT1", "v0", "v1", "x2n", "xres0", "xres1", "S", "pT"):
                c[n] = sb(n, [P, 4, 512])
            c["glu"], c["att"] = sb("glu", [P, 2, 512]), sb("att", [P, P])
            c["xin"] = c["x2n"]
            for n in ("qT", "kT", "v", "xres"):
                c[n] = [c[n + "0"], c[n + "1"]]
            c["bqk"] = sb("bqk", [P, 2 * HG])
            c["bv"], c["bo"], c["maskrow"] = sb("bv", [P, D]), sb("bo", [P, D]), sb("maskrow", [P, SEQ])
            c["ebias"] = sb("ebias", [P, E])
            c["ones"], c["before"] = sb("ones", [P, P]), sb("before", [P, P])
            c["nmax"], c["den"] = sb("nmax", [P, GH]), sb("den", [P, GH])
            c["rden"], c["rdenT"] = sb("rden", [P, GH, HD]), sb("rdenT", [P, P])
            c["half"] = sb("half", [P, 1])
            c["stats1"], c["stats2"] = sb("stats1", [P, TT, 6]), sb("stats2", [P, TT, 6])
            c["mv1"], c["mv2"] = sb("mv1", [P, TT, 2]), sb("mv2", [P, TT, 2])
            for n in ("sig", "sc", "sel", "wgt", "carry4", "eoff"):
                c[n] = sb(n, [P, TT, E])
            c["hi"], c["lo"] = sb("hi", [P, TT * NG, 2]), sb("lo", [P, TT * NG, 2])
            c["m1"], c["m2"] = sb("m1", [P, TT * NG]), sb("m2", [P, TT * NG])
            c["gval"], c["gout"] = sb("gval", [P, TT, NG + 8 - TOPG]), sb("gout", [P, TT, NG + 8 - TOPG])
            c["mval"], c["eout"] = sb("mval", [P, TT, E + 8 - TOPK]), sb("eout", [P, TT, E + 8 - TOPK])
            c["grep"], c["erep"], c["top8"] = sb("grep", [P, TT, 8]), sb("erep", [P, TT, 8]), sb("top8", [P, TT, 8])
            c["gmask"] = sb("gmask", [P, TT, NG])
            c["carry"], c["count"], c["wsum"] = sb("carry", [P, E]), sb("count", [P, E]), sb("wsum", [P, TT])
            c["eq"] = sb("eq", [P, TT, TOPK, E])
            c["rec"] = sb("rec", [P, TT, TOPK, 2])
            c["none"], c["idxf"], c["idx"] = sb("none", [P, TT, TOPK]), sb("idxf", [P, TT, TOPK]), sb("idx", [P, TT, TOPK], I32)
            c["tok"], c["tok_i"] = sb("tok", [P, TT]), sb("tok_i", [P, TT], I32)
            c["eoff_i"] = c["wgt"][:, :, :].bitcast(I32)
            c["fill_i"] = c["S"][0:E, 3, 0:CAPP].bitcast(I32).rearrange("e (c p) -> e c p", p=P)
            setup(nc, a, c, ps)
            sequences(nc, a, c, ps)
        with ExitStack() as second:
            def sb2(name, shape, dt=F32):
                return second.enter_context(nc.sbuf_tensor(name, shape, dt))

            nr = E * CS
            e_ = {"ident": ident, "table": sb2("table", [nr, 2 * P]), "split": sb2("split", [nr, 2, P]),
                  "tok": sb2("slot_tok", [P, nr], I32), "w": sb2("slot_w", [P, nr]),
                  "xT": [sb2(f"ex_xT_{h}", [P, DK, CAP], F16) for h in ("hi", "lo")],
                  "hT": [sb2(f"ex_hT_{h}", [P, JB, CAP], F16) for h in ("hi", "lo")],
                  "glu": sb2("ex_glu", [P, JB, CAP])}
            for n, shape in (("wg", [P, DK, IE]), ("wu", [P, DK, IE]), ("wd", [P, JB, D])):
                e_["raw_" + n] = [sb2(f"ex_raw_{n}{q}", shape) for q in range(2)]
                e_[n] = [[sb2(f"ex_{n}{q}_{h}", shape, F16) for h in ("hi", "lo")] for q in range(2)]
            for n, shape, dt in (("xg", [P, CS, D], F32), ("y", [P, CS, D], F32), ("gidx", [P, CS], I32),
                                 ("sidx", [P, CS], I32), ("wcol", [P, CS], F32)):
                e_[n] = [sb2(f"ex_{n}{q}", shape, dt) for q in range(2)]
            experts(nc, a, e_, ps)


_INS = {"x": "L0_attn_x", "Wqkv": "L0_attn_Wqkv", "bqkv": "L0_attn_bqkv", "Wo": "L0_attn_Wo", "bo": "L0_attn_bo",
        "router_w": "L0_ffn_router_w", "e_bias": "L0_ffn_e_bias", "W_gate": "L0_ffn_W_gate", "W_up": "L0_ffn_W_up",
        "W_down": "L0_ffn_W_down", "shared_gate": "L0_ffn_shared_gate", "shared_up": "L0_ffn_shared_up",
        "shared_down": "L0_ffn_shared_down"}


def kernel(**inputs):
    import concourse.bacc as _bacc
    from concourse.bass_utils import run_bass_kernel_spmd as _run

    nc = _bacc.Bacc("TRN2", target_bir_lowering=False, num_devices=1)
    arrays, a = {}, {}
    for short, name in _INS.items():
        arrays[f"in_{short}"] = np.ascontiguousarray(inputs[name])
        a[short] = nc.dram_tensor(f"in_{short}", arrays[f"in_{short}"].shape, F32, kind="ExternalInput").ap()
    a["out"] = nc.dram_tensor("out_0", (TOKENS + CAPP, D), F32, kind="ExternalOutput").ap()
    a["x2n"] = nc.dram_tensor("x2n_dram", (TOKENS + CAPP, D), F32, kind="Internal").ap()
    a["slots"] = nc.dram_tensor("slots_dram", (SLOTS, 2), F32, kind="Internal").ap()
    transformer_block(nc, a)
    r = _run(nc, [arrays], core_ids=[0])
    return np.asarray(r.results[0]["out_0"])[:TOKENS].reshape(BATCH, SEQ, D)
```

```python
from contextlib import ExitStack

import numpy as np

import concourse.bass as bass
from concourse import mybir

F32 = mybir.dt.float32
F16 = mybir.dt.float16
I32 = mybir.dt.int32
ALU = mybir.AluOpType
ACT = mybir.ActivationFunctionType
AX = mybir.AxisListType

P = 128
BATCH, SEQ, D = 16, 512, 512
TOKENS = BATCH * SEQ
TT = SEQ // P
DK = D // P
HEADS, HD = 16, 32
GH = P // HD
HG = HEADS // GH
STEPS = HG * TT
SCALE = float(HD) ** -0.5
EPS = 1e-5
I2 = 512
IB = I2 // P
E, TOPK, NG, TOPG = 32, 4, 8, 3
GE = E // NG
ROUTE_SCALE = 2.5
CAP = (5 * TOKENS // 4 + E - 1) // E
CS = -(-CAP // P)
CAPP = CS * P
LASTC = CAP - (CS - 1) * P
SLOTS = E * CAPP
IE = 256
JB = IE // P
WS = 2.0 ** 6
XS = 2.0 ** 10
AS = 2.0 ** 8
QS = 2.0 ** 5
HS = 2.0 ** 4
MASKED = -10000.0 / SCALE * QS * QS
SROWS = 3 * HD
SHG = HG // 2
STACK_DMAS = 2 * 3 * GH
DENSE = 3
LOW, HIGH = -3.0e38, 3.0e38

GROUPS = ([g for t in range(TT) for g in (("xT", t, 1), ("out", t, 4))]
          + [(w, g, 4) for g in range(HG) for w in ("q", "k")]
          + [("v", 0, 4)] + [g for t in range(1, TT) for g in (("v", t, 4), ("x2T", t - 1, 1))]
          + [("x2T", TT - 1, 1), ("router", 0, 4)]
          + [(w, j, 4) for j in range(IB - 2) for w in ("gate", "up")]
          + [("gate", IB - 2, 4), ("pos", 0, 1), ("up", IB - 2, 4)] + [(w, IB - 1, 4) for w in ("gate", "up")]
          + [("down", t, 4) for t in range(TT)])


def last_slot(kind, n):
    at = 0
    for k, m, pieces in GROUPS:
        at += pieces
        if (k, m) == (kind, n):
            return at - 1


LN2_SLOT = {last_slot("out", t) + 3: t for t in range(TT)}
STAT_SLOT = {last_slot("router", 0) + at: t for t, at in enumerate((36, 40, 44, 47))}
LN1_SLOT = {slot + 4: t for slot, t in STAT_SLOT.items()}
ROUTE_SLOT = {last_slot("router", 0) + at: n for n, at in enumerate((1, 5, 6, 7, 13, 14))}
DEST_SLOT = {last_slot("pos", 0) + at: n for n, at in enumerate((0, 1, 2, 3))}
QK_SLOT = {last_slot(w, g) + 2: (w, g) for g in range(HG) for w in ("q", "k")}
T_SLOT = 3
DEN_SLOT = 6
LAST_H = last_slot("up", IB - 1) + 1
PROJ = ("xT", "q", "k", "v")
N_PROJ = sum(k in PROJ for k, _, _ in GROUPS)
N_TAIL = len(GROUPS) - N_PROJ
SLOTS_STEP = 8


def schedule(proj, tail):
    out, counts, at = [], {True: 0, False: 0}, 0
    for kind, n, pieces in GROUPS:
        of_proj = kind in PROJ
        if (proj if of_proj else tail):
            out.append((kind, n, at, pieces, len(out), counts[of_proj]))
            counts[of_proj] += 1
        at += pieces
    assert at <= STEPS * SLOTS_STEP
    return out


ALL = slice(None)


def both(pair, *index):
    return tuple(x[index] for x in pair)


def product(pe, out, w, x, start, stop):
    pe.matmul(out, w[0], x[0], start=start, stop=False)
    pe.matmul(out, w[0], x[1], start=False, stop=False)
    return pe.matmul(out, w[1], x[0], start=False, stop=stop)


def setup(nc, a, c, ps):
    with ExitStack() as ctx:
        sem = lambda n: ctx.enter_context(nc.semaphore(n))
        loaded = [sem(f"setup_loaded{i}") for i in range(5)]
        direct_loaded = sem("setup_direct_loaded")
        zeroed = sem("setup_zeroed")
        filled = sem("setup_filled")
        made, ident_made = sem("setup_made"), sem("setup_ident_made")
        tables_written = sem("setup_tables_written")
        tr_done = sem("setup_tr_done")
        bank_free = [sem("setup_bank_free0"), sem("setup_bank_free1")]
        block = ctx.enter_context(nc.Block())
        raw_loaded = [sem(f"setup_raw_loaded{i}") for i in range(4)]
        hi_ready = sem("setup_hi_ready")
        halves_of = lambda name: [c[name][:, h * 2:(h + 1) * 2, :, :].rearrange("p g h n -> p (g h n)").bitcast(F32)
                                  .rearrange("p (k n) -> p k n", k=DK) for h in range(2)]
        raw = [*halves_of("stack_q"), c["v0"]]
        dst = [c["sgT"], c["suT"], c["sdT"]]
        rw_raw = c["xres0"][0:E, 0, :]
        bqk_raw = c["xres0"][0:2 * HG, 1, 0:P]
        plain = [*halves_of("stack_k"), c["v1"], c["pT"]]
        split = [both(c["wqkv"], ALL, ALL, slice(n * D, (n + 1) * D)) for n in range(3)]
        split.append(both(c["wo"], ALL, ALL, ALL))
        jobs = [(w, k) for w in range(3) for k in range(DK)] + [(3, 0), (4, 0)]
        order = [("job", n) for n in range(2 * DK)] + [("plain", 0)] + [("job", n) for n in range(2 * DK, 3 * DK + 1)]
        order += [("plain", 1), ("job", 3 * DK + 1)] + [("plain", n) for n in (2, 3)]

        @block.sync
        def _(sp):
            for w, name in enumerate(("shared_gate", "shared_up", "shared_down")):
                sp.dma_start(raw[w][:, :, :], a[name].rearrange("(i p) d -> p i d", p=P)).then_inc(loaded[w], 16)
            sp.dma_start(rw_raw, a["router_w"]).then_inc(loaded[3], 16)
            sp.dma_start(bqk_raw, a["bqkv"][0:2 * D].rearrange("(f p) -> f p", p=P)).then_inc(loaded[4], 16)
            for n in range(4):
                of = a["Wqkv"][:, n * D:(n + 1) * D] if n < 3 else a["Wo"]
                sp.dma_start(plain[n][:, :, :], of.rearrange("(k p) n -> p k n", p=P)).then_inc(raw_loaded[n], 16)
            direct = [
                (c["bv"][:, :], a["bqkv"][2 * D:3 * D].rearrange("(o n) -> o n", o=1).broadcast_to([P, D])),
                (c["bo"][:, :], a["bo"].rearrange("(o n) -> o n", o=1).broadcast_to([P, D])),
                (c["ebias"][:, :], a["e_bias"].rearrange("(o n) -> o n", o=1).broadcast_to([P, E])),
                (c["xin"][:, :, :], a["x"].rearrange("b (t p) d -> b p t d", p=P)[0]),
            ]
            for to, of in direct:
                sp.dma_start(to, of).then_inc(direct_loaded, 16)
            sp.wait_ge(direct_loaded, 16 * len(direct))
            sp.wait_ge(filled, 2)
            sp.dma_start(a["slots"].rearrange("(e s) w -> e (s w)", e=E),
                         c["S"][0:E, 0:2, :].rearrange("e a n -> e (a n)")[:, 0:2 * CAPP]).then_inc(tables_written, 16)
            for name in ("x2n", "out"):
                for n in range(CS):
                    sp.dma_start(a[name][TOKENS + n * P:TOKENS + (n + 1) * P, :], c["S"][:, 2, :]).then_inc(tables_written, 16)
            sp.wait_ge(tables_written, 16 * (1 + 2 * CS))

        @block.gpsimd
        def _(pool):
            pool.memset(c["ident"][:, :], 0.0).then_inc(zeroed, 1)
            pool.wait_ge(zeroed, 1)
            pool.affine_select(out=c["ident"][:, :], in_=c["ident"][:, :], compare_op=ALU.not_equal, fill=1.0,
                               base=0, pattern=[[-1, P]], channel_multiplier=1).then_inc(ident_made, 1)
            pool.memset(c["maskrow"][:, :], 0.0)
            pool.memset(c["before"][:, :], 1.0)
            pool.memset(c["ones"][:, :], 1.0)
            pool.memset(c["half"][:, :], -0.5)
            pool.memset(c["carry"][:, :], 0.0)
            pool.memset(c["gval"][:, :, :], LOW)
            pool.memset(c["grep"][:, :, :], LOW)
            pool.memset(c["mval"][:, :, :], LOW)
            pool.memset(c["erep"][:, :, :], LOW)
            pool.memset(c["S"][:, :, :], 0.0).then_inc(zeroed, 1)
            pool.wait_ge(zeroed, 2)
            tri = c["maskrow"][:, SEQ - P:SEQ]
            pool.affine_select(out=tri, in_=tri, compare_op=ALU.is_ge, fill=MASKED,
                               base=0, pattern=[[-1, P]], channel_multiplier=1)
            pool.affine_select(out=c["before"][:, :], in_=c["before"][:, :], compare_op=ALU.is_gt, fill=0.0,
                               base=0, pattern=[[1, P]], channel_multiplier=-1)
            pool.iota(c["tok_i"][:, :], pattern=[[P, TT]], base=0, channel_multiplier=1)
            pool.iota(c["eoff_i"][:, :, :], pattern=[[0, TT], [CAPP, E]], base=1, channel_multiplier=0)
            pool.iota(c["fill_i"], pattern=[[P, CS], [1, P]], base=TOKENS, channel_multiplier=0).then_inc(made, 1)

        def halves(w, k, bank):
            if w < 3:
                return both(dst[w], ALL, k, ALL), bank[:, :]
            return both(c["rwT"], ALL, ALL, ALL), bank[:, 0:DK * E].rearrange("p (k e) -> p k e", k=DK)

        @block.vector
        def _(dve):
            dve.wait_ge(made, 1)
            dve.tensor_copy(c["tok"][:, :], c["tok_i"][:, :])
            dve.tensor_copy(c["eoff"][:, :, :], c["eoff_i"][:, :, :]).then_inc(filled, 1)
            empty = c["S"][0:E, 0:2, :].rearrange("e a n -> e (a n)")[:, 0:2 * CAPP].rearrange("e (s w) -> e s w", w=2)
            dve.tensor_copy(empty[:, :, 0], c["fill_i"].rearrange("e c p -> e (c p)")).then_inc(filled, 1)
            his = 0
            for what, n in order:
                if what == "plain":
                    his += 1
                    dve.wait_ge(hi_ready, his)
                    dve.scalar_tensor_tensor(split[n][1], plain[n][:, :, :], WS, split[n][0], ALU.mult, ALU.subtract)
                    continue
                w, k = jobs[n]
                bank = ps["dense"][n % 2]
                if w < 4:
                    his += 1
                    to, of = halves(w, k, bank)
                    dve.wait_ge(hi_ready, his)
                    dve.scalar_tensor_tensor(to[1], of, WS, to[0], ALU.mult, ALU.subtract).then_inc(bank_free[n % 2], 1)
                else:
                    dve.wait_ge(tr_done, n + 1)
                    dve.tensor_scalar_mul(c["bqk"][:, :], bank[:, 0:2 * HG], QS).then_inc(bank_free[n % 2], 1)

        @block.scalar
        def _(act):
            for what, n in order:
                if what == "plain":
                    act.wait_ge(raw_loaded[n], 16)
                    act.activation(split[n][0], plain[n][:, :, :], ACT.Copy, scale=WS).then_inc(hi_ready, 1)
                elif jobs[n][0] < 4:
                    act.wait_ge(tr_done, n + 1)
                    to, of = halves(*jobs[n], ps["dense"][n % 2])
                    act.activation(to[0], of, ACT.Copy, scale=WS).then_inc(hi_ready, 1)

        @block.tensor
        def _(pe):
            pe.wait_ge(ident_made, 1)
            for n, (w, k) in enumerate(jobs):
                if k == 0:
                    pe.wait_ge(loaded[w], 16)
                if n >= 2:
                    pe.wait_ge(bank_free[n % 2], n // 2)
                bank = ps["dense"][n % 2]
                for i in range(4 if w < 4 else 1):
                    if w == 4:
                        last = pe.transpose(bank[:, 0:2 * HG], bqk_raw, c["ident"][0:2 * HG, 0:2 * HG])
                    elif w < 3:
                        last = pe.transpose(bank[:, i * P:(i + 1) * P], raw[w][:, i, k * P:(k + 1) * P], c["ident"][:, :])
                    else:
                        last = pe.transpose(bank[:, i * E:(i + 1) * E], rw_raw[:, i * P:(i + 1) * P], c["ident"][0:E, 0:E])
                last.then_inc(tr_done, 1)


def sequences(nc, a, c, ps):
    with ExitStack() as ctx:
        sem = lambda n: ctx.enter_context(nc.semaphore(n))
        xin_loaded, xres_loaded = sem("xin_loaded"), sem("xres_loaded")
        x2n_stored, out_stored = sem("x2n_stored"), sem("out_stored")
        slots_scattered = sem("slots_scattered")
        proj_done, tail_done = sem("proj_done"), sem("tail_done")
        x1_ready, gate_used, pos_used = sem("x1_ready"), sem("gate_used"), sem("pos_used")
        xT_ready, v_ready, x2T_ready = sem("xT_ready"), sem("v_ready"), sem("x2T_ready")
        qk_read, qk_split = sem("qk_read"), sem("qk_split")
        stacked = [sem("stacked0"), sem("stacked1")]
        tanh_ready, glu_ready = sem("tanh_ready"), sem("glu_ready")
        xT_hi, x2T_hi, hT_hi, h_ready = sem("xT_hi"), sem("x2T_hi"), sem("hT_hi"), sem("h_ready")
        scores_done, masked_done, exp_done = sem("scores_done"), sem("masked_done"), sem("exp_done")
        pT_done, pT_copied, rden_ready = sem("pT_done"), sem("pT_copied"), sem("rden_ready")
        o_done, o_used = sem("o_done"), sem("o_used")
        ln1_stats, ln1_normed = sem("ln1_stats"), sem("ln1_normed")
        ln2_stats, ln2_normed = sem("ln2_stats"), sem("ln2_normed")
        rstd1_ready, rstd2_ready = sem("rstd1_ready"), sem("rstd2_ready")
        xres_biased, out_ready = sem("xres_biased"), sem("out_ready")
        sig_exp, sel_ready, dest_ready = sem("sig_exp"), sem("sel_ready"), sem("dest_ready")
        dve_chain, settled = sem("dve_chain"), sem("settled")
        block = ctx.enter_context(nc.Block())

        x_v = a["x"].rearrange("b (t p) d -> b p t d", p=P)
        x2n_v = a["x2n"][0:TOKENS, :].rearrange("(b t p) d -> b p t d", b=BATCH, p=P)
        out_v = a["out"][0:TOKENS, :].rearrange("(b t p) d -> b p t d", b=BATCH, p=P)

        def turns(eng, turn):
            turn(0, 0, True, False, False)
            turn(1, 1, True, True, False)
            with eng.Fori(0, (BATCH - 2) // 2) as pair:
                turn(pair * 2 + 2, 0, True, True, True)
                turn(pair * 2 + 3, 1, True, True, True)
            turn(BATCH, 0, False, True, True)
            turn(BATCH + 1, 1, False, False, True)

        def settle(eng):
            eng.sem_inc(settled, 1)

        def done_wait(eng, i, kind, at):
            if kind in PROJ:
                eng.wait_ge(proj_done, i * N_PROJ + at + 1)
            else:
                eng.wait_ge(tail_done, (i - 2) * N_TAIL + at + 1)

        def read_wait(eng, i, kind, m):
            b = i - 2
            if kind == "out":
                eng.wait_ge(x1_ready, b * TT + m + 1)
            elif kind == "xT":
                eng.wait_ge(xT_ready, i * TT + m + 1)
            elif kind in ("q", "k"):
                eng.wait_ge(qk_read, (i * 2 * HG + 2 * m + (kind == "k") + 1) * 2)
            elif kind == "v":
                eng.wait_ge(v_ready, i * TT + m + 1)
            elif kind == "x2T":
                eng.wait_ge(x2T_ready, b * TT + m + 1)
            elif kind == "router":
                eng.wait_ge(sig_exp, b + 1)
            elif kind == "gate":
                eng.wait_ge(gate_used, b * IB + m + 1)
            elif kind == "up":
                eng.wait_ge(glu_ready, b * IB + m + 1)
            elif kind == "pos":
                eng.wait_ge(pos_used, b + 1)
            elif kind == "down":
                eng.wait_ge(out_ready, (b + 1) * TT + m + 1)

        @block.sync
        def _(sp):
            def stack(half):
                groups = slice(half * SHG, (half + 1) * SHG)
                for name, parts in (("q", (0, 1, 0)), ("k", (0, 0, 1))):
                    for n, part in enumerate(parts):
                        for h in range(GH):
                            sp.dma_start(c["stack_" + name][n * HD:(n + 1) * HD, groups, h, :],
                                         c["split_" + name][part][h * HD:(h + 1) * HD, groups, :]).then_inc(stacked[half], 16)

            def turn(i, par, proj, attn, fin):
                b = i - 2
                if attn:
                    if fin:
                        sp.wait_ge(scores_done, (i - 1) * STEPS)
                        settle(sp)
                    stack(1)
                    if fin:
                        sp.wait_ge(xres_biased, (i - 1) * TT)
                        settle(sp)
                    sp.dma_start(c["xres"][1 - par][:, :, :], x_v[i - 1]).then_inc(xres_loaded, 16)
                if fin:
                    sp.wait_ge(ln2_normed, (b + 1) * TT)
                    sp.dma_start(x2n_v[b], c["x2n"][:, :, :]).then_inc(x2n_stored, 16)
                if proj:
                    sp.wait_ge(qk_split, (i + 1) * 2 * HG)
                    settle(sp)
                    if attn:
                        sp.wait_ge(scores_done, (i - 1) * STEPS + STEPS // 2)
                        settle(sp)
                    stack(0)
                    sp.wait_ge(proj_done, i * N_PROJ + TT)
                    settle(sp)
                    if fin:
                        sp.wait_ge(x2T_ready, (b + 1) * TT)
                        settle(sp)
                        sp.wait_ge(x2n_stored, (b + 1) * 16)
                        settle(sp)
                    sp.dma_start(c["xin"][:, :, :], x_v[(i + 1) % BATCH]).then_inc(xin_loaded, 16)
                if fin:
                    sp.wait_ge(out_ready, (b + 2) * TT)
                    sp.dma_start(out_v[b], c["xres"][par][:, :, :]).then_inc(out_stored, 16)
                    sp.wait_ge(out_stored, (b + 1) * 16)
                    settle(sp)

            turns(sp, turn)
            sp.wait_ge(x2n_stored, 16 * BATCH)
            sp.wait_ge(out_stored, 16 * BATCH)

        @block.tensor
        def _(pe):
            ident = c["ident"][:, :]

            def dense(i, par, slot, groups, fin):
                hit = [g for g in groups if g[2] <= slot < g[2] + g[3]]
                if not hit:
                    return
                kind, m, first, pieces, pos, at = hit[0]
                k, b = slot - first, i - 2
                bank = ps["dense"][pos % DENSE]
                if k == 0 and pos >= DENSE:
                    read_wait(pe, i, *groups[pos - DENSE][0:2])
                elif k == 0 and not (isinstance(i, int) and i == 0):
                    pe.wait_ge(v_ready, min(i, BATCH) * TT if isinstance(i, int) else i * TT)
                    if fin:
                        full = not isinstance(i, int) or i <= BATCH
                        pe.wait_ge(out_ready, (b + 1) * TT - (full and pos == 0))
                blk = slice(m * P, (m + 1) * P)
                if kind == "out":
                    if k == 0:
                        pe.wait_ge(o_used, b * STEPS + STEPS - TT + m + 1)
                    last = product(pe, bank[:, :], both(c["aT"], ALL, k, blk), both(c["wo"], ALL, k, ALL), k == 0, k == DK - 1)
                elif kind == "xT":
                    pe.wait_ge(ln1_normed, i * TT + m + 1)
                    for j in range(DK):
                        last = pe.transpose(bank[:, j * P:(j + 1) * P], c["xin"][:, m, j * P:(j + 1) * P], ident)
                elif kind in ("q", "k"):
                    if k == 0 and kind == "q" and m == 0:
                        pe.wait_ge(xT_ready, (i + 1) * TT)
                    off = (kind == "k") * D + m * P
                    last = product(pe, bank[:, :], both(c["wqkv"], ALL, k, slice(off, off + P)), both(c["xT"], ALL, k, ALL), k == 0, k == DK - 1)
                elif kind == "v":
                    last = product(pe, bank[:, :], both(c["xT"], ALL, k, blk), both(c["wqkv"], ALL, k, slice(2 * D, 3 * D)), k == 0, k == DK - 1)
                elif kind == "x2T":
                    pe.wait_ge(ln2_normed, b * TT + m + 1)
                    for j in range(DK):
                        last = pe.transpose(bank[:, j * P:(j + 1) * P], c["x2n"][:, m, j * P:(j + 1) * P], ident)
                elif kind == "router":
                    pe.wait_ge(x2T_ready, b * TT + k + 1)
                    for j in range(DK):
                        last = product(pe, bank[:, k * E:(k + 1) * E], both(c["xT"], ALL, j, slice(k * P, (k + 1) * P)),
                                       both(c["rwT"], ALL, j, ALL), j == 0, j == DK - 1)
                elif kind in ("gate", "up"):
                    w = c["sgT"] if kind == "gate" else c["suT"]
                    last = product(pe, bank[:, :], both(w, ALL, k, blk), both(c["xT"], ALL, k, ALL), k == 0, k == DK - 1)
                elif kind == "pos":
                    pe.wait_ge(sel_ready, b + 1)
                    sel = c["sel"][:, :, :].rearrange("p t e -> p (t e)")
                    n = TT * E
                    pe.matmul(bank[:, 0:n], c["ones"][:, :], c["carry4"][:, :, :].rearrange("p t e -> p (t e)"), start=True, stop=False)
                    pe.matmul(bank[:, 0:n], c["before"][:, :], sel, start=False, stop=False)
                    for s in range(1, TT):
                        last = pe.matmul(bank[:, s * E:n], c["ones"][:, :], sel[:, 0:n - s * E], start=False, stop=s == TT - 1)
                elif kind == "down":
                    if m == 0:
                        pe.wait_ge(h_ready, b * IB + k + 1)
                    last = product(pe, bank[:, :], both(c["hT"], ALL, k, blk), both(c["sdT"], ALL, k, ALL), k == 0, k == IB - 1)
                if k == pieces - 1:
                    last.then_inc(proj_done if kind in PROJ else tail_done, 1)

            def scores(i, s):
                hg, qt = divmod(s, TT)
                g = (i - 1) * STEPS + s
                if s % (STEPS // 2) == 0:
                    pe.wait_ge(stacked[hg // SHG], i * STACK_DMAS * 16)
                for h in range(GH):
                    if not (isinstance(i, int) and i == 1 and s == 0):
                        pe.wait_ge(pT_copied, (g - 1) * GH + h + 1)
                    last = pe.matmul(ps["scores"][h][:, 0:(qt + 1) * P], c["stack_q"][0:SROWS, hg, h, qt * P:(qt + 1) * P],
                                     c["stack_k"][0:SROWS, hg, h, 0:(qt + 1) * P], start=True, stop=True)
                last.then_inc(scores_done, 1)

            def transpose_probs(i, s, h):
                g = (i - 1) * STEPS + s
                pe.wait_ge(exp_done, g * GH + h + 1)
                for kt in range(s % TT + 1):
                    last = pe.transpose(ps["scores"][h][:, kt * P:(kt + 1) * P], c["S"][:, h, kt * P:(kt + 1) * P], ident)
                last.then_inc(pT_done, 1)

            def values(i, par, s):
                hg, qt = divmod(s, TT)
                g = (i - 1) * STEPS + s
                if s == 0:
                    pe.wait_ge(v_ready, i * TT)
                pe.wait_ge(pT_copied, (g + 1) * GH)
                if not (isinstance(i, int) and i == 1 and s == 0):
                    pe.wait_ge(o_used, g)
                for kt in range(qt + 1):
                    for h in range(GH):
                        rows = slice(h * HD, (h + 1) * HD)
                        pe.matmul(ps["o"][rows, 0:P], c["v"][par][:, kt, hg * P + h * HD:hg * P + (h + 1) * HD],
                                  c["pT"][:, h, kt * P:(kt + 1) * P], start=kt == 0, stop=kt == qt)

            def denominators_T(i, s):
                g = (i - 1) * STEPS + s
                pe.wait_ge(rden_ready, g + 1)
                pe.transpose(ps["o"][:, P:2 * P], c["rden"][:, :, :].rearrange("p h d -> p (h d)"), ident).then_inc(o_done, 1)

            def turn(i, par, proj, attn, fin):
                groups = schedule(proj, fin)
                for s in range(STEPS):
                    slot = s * SLOTS_STEP
                    if attn:
                        scores(i, s)
                    dense(i, par, slot, groups, fin)
                    if s == 0 and fin:
                        values(i - 1, par, STEPS - 1)
                    if s > 0 and attn:
                        values(i, 1 - par, s - 1)
                    for n in range(1, SLOTS_STEP):
                        if n == 3 and s == 0 and fin:
                            denominators_T(i - 1, STEPS - 1)
                        if n == 3 and s > 0 and attn:
                            denominators_T(i, s - 1)
                        if attn and 0 <= n - T_SLOT < GH:
                            transpose_probs(i, s, n - T_SLOT)
                        dense(i, par, slot + n, groups, fin)

            turns(pe, turn)

        @block.scalar
        def _(act):
            def copies(i, proj, slot, groups):
                hit = [g for g in groups if g[2] + g[3] - 1 == slot]
                if not hit:
                    return
                kind, m, _, _, pos, at = hit[0]
                bank = ps["dense"][pos % DENSE]
                if kind in ("xT", "x2T"):
                    done_wait(act, i, kind, at)
                    act.activation(c["xT"][0][:, :, m * P:(m + 1) * P], bank[:, :].rearrange("p (k t) -> p k t", k=DK),
                                   ACT.Copy, scale=XS).then_inc(xT_hi if kind == "xT" else x2T_hi, 1)
                elif kind in ("q", "k"):
                    f, n = (kind == "k") * HG + m, 2 * m + (kind == "k")
                    if not (isinstance(i, int) and i == 0):
                        act.wait_ge(stacked[m // SHG], i * STACK_DMAS * 16)
                    if n >= 2:
                        act.wait_ge(qk_split, i * 2 * HG + n - 1)
                    done_wait(act, i, kind, at)
                    for to in (c["glu"][:, n % 2, :], c["split_" + kind][0][:, m, :]):
                        act.activation(to, bank[:, :], ACT.Identity, bias=c["bqk"][:, f:f + 1],
                                       scale=QS / (XS * WS)).then_inc(qk_read, 1)
                elif kind == "router":
                    done_wait(act, i, kind, at)
                    act.activation(c["sig"][:, :, :].rearrange("p t e -> p (t e)"), bank[:, 0:TT * E], ACT.Exp,
                                   scale=-1.0 / (XS * WS)).then_inc(sig_exp, 1)
                elif kind == "gate":
                    done_wait(act, i, kind, at)
                    if m >= 2:
                        act.wait_ge(h_ready, (i - 2) * IB + m - 1)
                    elif proj:
                        act.wait_ge(qk_split, (i + 1) * 2 * HG)
                    act.activation(c["glu"][:, m % 2, :], bank[:, :], ACT.Tanh, scale=0.5 / (XS * WS)).then_inc(tanh_ready, 1)
                if kind == "up" and m > 0:
                    h_hi(i, m - 1)

            def norm(x, to, mv, rstd, count, done):
                act.wait_ge(rstd, count * 3)
                act.activation(to, x, ACT.Identity, bias=mv[:, 0:1], scale=mv[:, 1:2]).then_inc(done, 1)

            def norms(i, par, slot, proj, fin):
                if proj and slot in LN1_SLOT:
                    norm1(i + 1, LN1_SLOT[slot])
                if fin and slot in LN2_SLOT:
                    t, b = LN2_SLOT[slot], i - 2
                    if isinstance(i, int) and i == BATCH and t == 0:
                        act.wait_ge(ln1_normed, (BATCH + 1) * TT)
                    norm(c["xres"][par][:, t, :], c["x2n"][:, t, :], c["mv2"][:, t, :], rstd2_ready, b * TT + t + 1, ln2_normed)
                if fin and slot == LAST_H:
                    h_hi(i, IB - 1)

            def norm1(j, t):
                norm(c["xin"][:, t, :], c["xin"][:, t, :], c["mv1"][:, t, :], rstd1_ready, j * TT + t + 1, ln1_normed)

            def h_hi(i, m):
                act.wait_ge(glu_ready, (i - 2) * IB + m + 1)
                act.activation(c["hT"][0][:, m, :], c["glu"][:, m % 2, :], ACT.Copy, scale=HS / (XS * WS) ** 2).then_inc(hT_hi, 1)

            def exp(i, s, h):
                g = (i - 1) * STEPS + s
                row = c["S"][:, h, 0:(s % TT + 1) * P]
                act.wait_ge(masked_done, g * GH + h + 1)
                act.activation(row, row, ACT.Exp, bias=c["nmax"][:, h:h + 1], scale=-1.0,
                               accum_out=c["den"][:, h:h + 1]).then_inc(exp_done, 1)

            def copy_probs(i, s, h):
                g = (i - 1) * STEPS + s
                n = (s % TT + 1) * P
                act.wait_ge(pT_done, g * GH + h + 1)
                act.activation(c["pT"][:, h, 0:n], ps["scores"][h][:, 0:n], ACT.Copy).then_inc(pT_copied, 1)

            def turn(i, par, proj, attn, fin):
                groups = schedule(proj, fin)
                for s in range(STEPS):
                    slot = s * SLOTS_STEP
                    if attn:
                        exp(i, s, 0)
                        exp(i, s, 1)
                    copies(i, proj, slot, groups)
                    norms(i, par, slot, proj, fin)
                    if attn:
                        exp(i, s, 2)
                        exp(i, s, 3)
                    copies(i, proj, slot + 1, groups)
                    norms(i, par, slot + 1, proj, fin)
                    copies(i, proj, slot + 2, groups)
                    norms(i, par, slot + 2, proj, fin)
                    for n in range(3, SLOTS_STEP):
                        if attn and 0 <= n - T_SLOT < GH:
                            copy_probs(i, s, n - T_SLOT)
                        copies(i, proj, slot + n, groups)
                        norms(i, par, slot + n, proj, fin)

            for t in range(TT):
                norm1(0, t)
            turns(act, turn)

        @block.vector
        def _(dve):
            chain = {"turn": 0, "links": 0}

            def link(ins):
                chain["links"] += 1
                ins.then_inc(dve_chain, 1)
                dve.wait_ge(dve_chain, chain["turn"] + chain["links"])

            def statistics(x, stats, mv):
                link(dve.bn_stats(stats, x))
                settle(dve)
                return dve.bn_aggr(mv, stats)

            flat = lambda t: t[:, :, :].rearrange("p t e -> p (t e)")

            def route_scores(i):
                dve.wait_ge(sig_exp, i - 1)
                link(dve.tensor_scalar_add(flat(c["sig"]), flat(c["sig"]), 1.0))
                link(dve.reciprocal(flat(c["sig"]), flat(c["sig"])))
                link(dve.tensor_tensor(c["sc"][:, :, :], c["sig"][:, :, :], c["ebias"][:, :].unsqueeze(1).broadcast_to([P, TT, E]), ALU.add))
                s4 = flat(c["sc"]).rearrange("p (g e) -> p g e", e=GE)
                hi, lo, m1, m2 = c["hi"][:, :, :], c["lo"][:, :, :], c["m1"][:, :], c["m2"][:, :]
                dve.tensor_tensor(hi, s4[:, :, 0:2], s4[:, :, 2:4], ALU.max)
                link(dve.tensor_tensor(lo, s4[:, :, 0:2], s4[:, :, 2:4], ALU.min))
                dve.tensor_tensor(m1, hi[:, :, 0], hi[:, :, 1], ALU.max)
                dve.tensor_tensor(m2, hi[:, :, 0], hi[:, :, 1], ALU.min)
                link(dve.tensor_tensor(lo[:, :, 0], lo[:, :, 0], lo[:, :, 1], ALU.max))
                link(dve.tensor_tensor(m2, m2, lo[:, :, 0], ALU.max))
                group = lambda t: t.rearrange("p (t g) -> p t g", t=TT)
                link(dve.tensor_tensor(c["gval"][:, :, 0:NG], group(m1), group(m2), ALU.add))

            def route_groups(i):
                settle(dve)
                for t in range(TT):
                    last = dve.max(c["top8"][:, t, :], c["gval"][:, t, 0:NG])
                link(last)
                link(dve.tensor_copy(c["grep"][:, :, 0:TOPG], c["top8"][:, :, 0:TOPG]))
                settle(dve)
                for t in range(TT):
                    last = dve.match_replace(c["gout"][:, t, :], c["grep"][:, t, :], c["gval"][:, t, :], HIGH)
                link(last)
                link(dve.tensor_scalar(c["gmask"][:, :, :], c["gout"][:, :, 0:NG], HIGH / 2, None, ALU.is_ge))

            def route_mask(i):
                for t in range(TT):
                    last = dve.tensor_tensor(c["mval"][:, t, 0:E].rearrange("p (g e) -> p g e", e=GE),
                                             c["sc"][:, t, :].rearrange("p (g e) -> p g e", e=GE),
                                             c["gmask"][:, t, :].unsqueeze(2).broadcast_to([P, NG, GE]), ALU.mult)
                link(last)
                link(dve.tensor_scalar_add(c["mval"][:, :, 0:E], c["mval"][:, :, 0:E], 0.0))

            def route_best(i):
                settle(dve)
                for t in range(TT):
                    last = dve.max(c["top8"][:, t, :], c["mval"][:, t, 0:E])
                link(last)
                link(dve.tensor_copy(c["erep"][:, :, 0:TOPK], c["top8"][:, :, 0:TOPK]))

            def route_select(i):
                settle(dve)
                for t in range(TT):
                    last = dve.match_replace(c["eout"][:, t, :], c["erep"][:, t, :], c["mval"][:, t, :], HIGH)
                link(last)
                link(dve.tensor_scalar(c["sel"][:, :, :], c["eout"][:, :, 0:E], HIGH / 2, None, ALU.is_ge))
                dve.tensor_copy(c["carry4"][:, :, :], c["carry"][:, :].unsqueeze(1).broadcast_to([P, TT, E])).then_inc(sel_ready, 1)

            def route_weights(i):
                link(dve.tensor_tensor(flat(c["wgt"]), flat(c["sig"]), flat(c["sel"]), ALU.mult))
                dve.tensor_reduce(c["count"][:, :], c["sel"][:, :, :].rearrange("p t e -> p e t"), AX.X, ALU.add)
                link(dve.tensor_reduce(c["wsum"][:, :], c["wgt"][:, :, :], AX.X, ALU.add))
                dve.tensor_tensor(c["carry"][:, :], c["carry"][:, :], c["count"][:, :], ALU.add)
                link(dve.tensor_scalar_add(c["wsum"][:, :], c["wsum"][:, :], 1e-20))
                link(dve.reciprocal(c["wsum"][:, :], c["wsum"][:, :]))
                link(dve.tensor_scalar_mul(c["wsum"][:, :], c["wsum"][:, :], ROUTE_SCALE / 2 / (HS * WS)))
                link(dve.tensor_tensor(c["wgt"][:, :, :], c["wgt"][:, :, :], c["wsum"][:, :].unsqueeze(2).broadcast_to([P, TT, E]), ALU.mult))

            ROUTE = (route_scores, route_groups, route_mask, route_best, route_select, route_weights)

            def dest_keys(i, bank):
                n = TT * E
                dve.scalar_tensor_tensor(flat(c["eout"])[:, 0:n], bank[:, 0:n], float(CAP), flat(c["sel"]), ALU.is_lt, ALU.mult)
                dve.tensor_tensor(flat(c["sc"]), bank[:, 0:n], flat(c["eoff"]), ALU.add).then_inc(pos_used, 1)
                dve.wait_ge(pos_used, i - 1)
                link(dve.tensor_tensor(flat(c["sc"]), flat(c["sc"]), flat(c["eout"])[:, 0:n], ALU.mult))

            def dest_slots(i, bank):
                settle(dve)
                for t in range(TT):
                    last = dve.max(c["top8"][:, t, :], c["sc"][:, t, :])
                link(last)
                for t in range(TT):
                    last = dve.tensor_tensor(c["eq"][:, t, :, :], c["sc"][:, t, :].unsqueeze(1).broadcast_to([P, TOPK, E]),
                                             c["top8"][:, t, 0:TOPK].unsqueeze(2).broadcast_to([P, TOPK, E]), ALU.is_equal)
                link(last)

            def dest_weights(i, bank):
                for t in range(TT):
                    last = dve.tensor_tensor(c["eq"][:, t, :, :], c["eq"][:, t, :, :],
                                             c["wgt"][:, t, :].unsqueeze(1).broadcast_to([P, TOPK, E]), ALU.mult)
                link(last)
                dve.tensor_reduce(c["rec"][:, :, :, 1], c["eq"][:, :, :, :], AX.X, ALU.add)
                dve.tensor_copy(c["rec"][:, :, :, 0], c["tok"][:, :].unsqueeze(2).broadcast_to([P, TT, TOPK]))

            def dest_records(i, bank):
                top = c["top8"][:, :, 0:TOPK]
                link(dve.tensor_scalar(c["none"][:, :, :], top, 0.5, float(1 << 20), ALU.is_lt, ALU.mult))
                link(dve.scalar_tensor_tensor(c["idxf"][:, :, :], top, -1.0, c["none"][:, :, :], ALU.add, ALU.add))
                link(dve.tensor_copy(c["idx"][:, :, :], c["idxf"][:, :, :]))
                dve.tensor_scalar_add(c["tok"][:, :], c["tok"][:, :], float(SEQ)).then_inc(dest_ready, 1)

            DESTINATIONS = (dest_keys, dest_slots, dest_weights, dest_records)

            def statistics1(j, t):
                if t == 0 and not (isinstance(j, int) and j == 0):
                    dve.wait_ge(xin_loaded, j * 16)
                statistics(c["xin"][:, t, :], c["stats1"][:, t, :], c["mv1"][:, t, :]).then_inc(ln1_stats, 1)

            def between(i, slot, groups, proj, fin):
                if fin and slot in ROUTE_SLOT:
                    ROUTE[ROUTE_SLOT[slot]](i)
                if fin and slot in DEST_SLOT:
                    bank, at = [(ps["dense"][g[4] % DENSE], g[5]) for g in groups if g[0] == "pos"][0]
                    if DEST_SLOT[slot] == 0:
                        done_wait(dve, i, "pos", at)
                    DESTINATIONS[DEST_SLOT[slot]](i, bank)
                if fin and slot == LAST_H:
                    h_lo(i, IB - 1)
                if proj and slot in QK_SLOT:
                    kind, m = QK_SLOT[slot]
                    n = 2 * m + (kind == "k")
                    dve.wait_ge(qk_read, (i * 2 * HG + n + 1) * 2)
                    hi, lo = both(c["split_" + kind], ALL, m, ALL)
                    dve.tensor_tensor(lo, c["glu"][:, n % 2, :], hi, ALU.subtract).then_inc(qk_split, 1)
                if proj and slot in STAT_SLOT:
                    statistics1(i + 1, STAT_SLOT[slot])

            def copies(i, par, slot, groups):
                hit = [g for g in groups if g[2] + g[3] - 1 == slot]
                if not hit:
                    return
                kind, m, _, _, pos, at = hit[0]
                bank, b = ps["dense"][pos % DENSE], i - 2
                if kind == "out":
                    x1 = c["xres"][par][:, m, :]
                    dve.wait_ge(xres_biased, (b + 1) * TT)
                    done_wait(dve, i, kind, at)
                    dve.scalar_tensor_tensor(x1, bank[:, :], 1.0 / (AS * WS), x1, ALU.mult, ALU.add).then_inc(x1_ready, 1)
                    dve.wait_ge(x1_ready, b * TT + m + 1)
                    statistics(x1, c["stats2"][:, m, :], c["mv2"][:, m, :]).then_inc(ln2_stats, 1)
                elif kind == "v":
                    done_wait(dve, i, kind, at)
                    dve.scalar_tensor_tensor(c["v"][par][:, m, :], bank[:, :], 1.0 / (XS * WS), c["bv"][:, :],
                                             ALU.mult, ALU.add).then_inc(v_ready, 1)
                elif kind in ("xT", "x2T"):
                    n = (i * TT + m + 1) if kind == "xT" else (b * TT + m + 1)
                    dve.wait_ge(xT_hi if kind == "xT" else x2T_hi, n)
                    cols = slice(m * P, (m + 1) * P)
                    dve.scalar_tensor_tensor(c["xT"][1][:, :, cols], bank[:, :].rearrange("p (k t) -> p k t", k=DK), XS,
                                             c["xT"][0][:, :, cols], ALU.mult, ALU.subtract
                                             ).then_inc(xT_ready if kind == "xT" else x2T_ready, 1)
                elif kind == "gate":
                    dve.wait_ge(tanh_ready, b * IB + m + 1)
                    glu = c["glu"][:, m % 2, :]
                    dve.scalar_tensor_tensor(glu, glu, 1.0, bank[:, :], ALU.add, ALU.mult).then_inc(gate_used, 1)
                elif kind == "up":
                    done_wait(dve, i, kind, at)
                    dve.wait_ge(gate_used, b * IB + m + 1)
                    glu = c["glu"][:, m % 2, :]
                    dve.tensor_tensor(glu, glu, bank[:, :], ALU.mult).then_inc(glu_ready, 1)
                    if m > 0:
                        h_lo(i, m - 1)
                elif kind == "down":
                    done_wait(dve, i, kind, at)
                    x1 = c["xres"][par][:, m, :]
                    dve.scalar_tensor_tensor(x1, bank[:, :], 0.5 / (HS * WS), x1, ALU.mult, ALU.add).then_inc(out_ready, 1)

            def h_lo(i, m):
                dve.wait_ge(hT_hi, (i - 2) * IB + m + 1)
                dve.scalar_tensor_tensor(c["hT"][1][:, m, :], c["glu"][:, m % 2, :], HS / (XS * WS) ** 2, c["hT"][0][:, m, :],
                                         ALU.mult, ALU.subtract).then_inc(h_ready, 1)

            def mask(i, s, h):
                g = (i - 1) * STEPS + s
                n = (s % TT + 1) * P
                if h == 0:
                    dve.wait_ge(scores_done, g + 1)
                settle(dve)
                dve.tensor_tensor_reduce(out=c["S"][:, h, 0:n], in0=ps["scores"][h][:, 0:n], in1=c["maskrow"][:, SEQ - n:SEQ],
                                         scale=-SCALE / (QS * QS), scalar=HIGH, op0=ALU.add, op1=ALU.min,
                                         accum_out=c["nmax"][:, h:h + 1]).then_inc(masked_done, 1)

            def denominators(i, s):
                g = (i - 1) * STEPS + s
                dve.wait_ge(exp_done, (g + 1) * GH)
                if not (isinstance(i, int) and i == 1 and s == 0):
                    dve.wait_ge(o_done, g)
                link(dve.reciprocal(c["den"][:, :], c["den"][:, :]))
                dve.tensor_copy(c["rden"][:, :, :], c["den"][:, :].unsqueeze(2).broadcast_to([P, GH, HD])).then_inc(rden_ready, 1)

            def normalise(i, s):
                hg, qt = divmod(s, TT)
                g = (i - 1) * STEPS + s
                dve.wait_ge(o_done, g + 1)
                cols = slice(qt * P, (qt + 1) * P)
                hi, lo = both(c["aT"], ALL, hg, cols)
                link(dve.tensor_copy(c["rdenT"][:, :], ps["o"][:, P:2 * P]))
                link(dve.scalar_tensor_tensor(c["att"][:, :], ps["o"][:, 0:P], AS, c["rdenT"][:, :], ALU.mult, ALU.mult))
                link(dve.tensor_copy(hi, c["att"][:, :]))
                dve.tensor_tensor(lo, c["att"][:, :], hi, ALU.subtract).then_inc(o_used, 1)

            def turn(i, par, proj, attn, fin):
                groups = schedule(proj, fin)
                chain["links"] = 0

                def place(slot):
                    copies(i, par, slot, groups)
                    between(i, slot, groups, proj, fin)

                for s in range(STEPS):
                    slot = s * SLOTS_STEP
                    if attn:
                        for h in range(GH):
                            mask(i, s, h)
                    place(slot)
                    if s == 0 and fin:
                        normalise(i - 1, STEPS - 1)
                    if s > 0 and attn:
                        normalise(i, s - 1)
                    for n in range(1, SLOTS_STEP):
                        if attn and n == DEN_SLOT:
                            denominators(i, s)
                        place(slot + n)
                chain["turn"] += chain["links"]

            def counted(i, par, proj, attn, fin):
                if isinstance(i, int):
                    turn(i, par, proj, attn, fin)
                else:
                    start = chain.setdefault("loop", chain["turn"])
                    chain["turn"] = (i - 2) * LINKS + start
                    turn(i, par, proj, attn, fin)
                    assert chain["links"] == LINKS, chain["links"]
                    chain["turn"] = start + (BATCH - 2) * LINKS

            dve.sem_inc(out_ready, TT)
            for t in range(TT):
                statistics1(0, t)
            chain["turn"] = chain["links"]
            turns(dve, counted)

        @block.gpsimd
        def _(pool):
            def scales(mv, rstd, count):
                settle(pool)
                pool.tensor_scalar(mv[:, 1:2], mv[:, 1:2], EPS, None, ALU.add).then_inc(rstd, 1)
                pool.wait_ge(rstd, count * 3 - 2)
                pool.tensor_tensor(mv[:, 1:2], mv[:, 1:2], c["half"][:, :], ALU.pow).then_inc(rstd, 1)
                pool.wait_ge(rstd, count * 3 - 1)
                settle(pool)
                pool.tensor_scalar(mv[:, 0:1], mv[:, 0:1], mv[:, 1:2], -1.0, ALU.mult, ALU.mult).then_inc(rstd, 1)

            def scales1(j, t):
                pool.wait_ge(ln1_stats, j * TT + t + 1)
                scales(c["mv1"][:, t, :], rstd1_ready, j * TT + t + 1)

            def turn(i, par, proj, attn, fin):
                b = i - 2
                for t in range(TT):
                    if fin:
                        pool.wait_ge(ln2_stats, b * TT + t + 1)
                        scales(c["mv2"][:, t, :], rstd2_ready, b * TT + t + 1)
                if attn:
                    pool.wait_ge(xres_loaded, i * 16)
                    for t in range(TT):
                        xt = c["xres"][1 - par][:, t, :]
                        pool.tensor_tensor(xt, xt, c["bo"][:, :], ALU.add).then_inc(xres_biased, 1)
                if fin:
                    pool.wait_ge(dest_ready, b + 1)
                    settle(pool)
                for t in range(TT):
                    if fin:
                        for k in range(TOPK):
                            pool.indirect_dma_start(
                                out=a["slots"], out_offset=bass.IndirectOffsetOnAxis(ap=c["idx"][:, t, k:k + 1], axis=0),
                                in_=c["rec"][:, t, k, :], in_offset=None, bounds_check=SLOTS - 1,
                                oob_is_err=False).then_inc(slots_scattered, 16)
                    if proj:
                        scales1(i + 1, t)
                if fin:
                    pool.wait_ge(x2n_stored, (b + 1) * 16)
                    settle(pool)
                    pool.wait_ge(slots_scattered, (b + 1) * (TT * TOPK * 16))
                    settle(pool)

            for t in range(TT):
                scales1(0, t)
            turns(pool, turn)


def experts(nc, a, e_, ps):
    with ExitStack() as ctx:
        sem = lambda n: ctx.enter_context(nc.semaphore(n))
        table_loaded, table_split, table_T, table_ready = sem("table_loaded"), sem("table_split"), sem("table_T"), sem("table_ready")
        gidx_ready, sidx_ready, wcol_ready = sem("gidx_ready"), sem("sidx_ready"), sem("wcol_ready")
        gathered = [sem("gathered0"), sem("gathered1")]
        w_loaded = [sem("w_loaded0"), sem("w_loaded1")]
        w_hi, w_ready = sem("w_hi"), sem("w_ready")
        xT_done, xT_hi, xT_copied = sem("ex_xT_done"), sem("ex_xT_hi"), sem("ex_xT_copied")
        gu_done, tanh_ready, glu_ready = sem("ex_gu_done"), sem("ex_tanh_ready"), sem("ex_glu_ready")
        h_hi, h_ready = sem("ex_h_hi"), sem("ex_h_ready")
        y_done, y_ready, y_added = sem("y_done"), sem("y_ready"), sem("y_added")
        settled = sem("ex_settled")
        block = ctx.enter_context(nc.Block())

        def settle(eng):
            eng.sem_inc(settled, 1)

        rows = lambda ch: P if ch < CS - 1 else LASTC
        WEIGHTS = (("wg", "W_gate"), ("wu", "W_up"), ("wd", "W_down"))
        arrived = lambda e, q, n: (e + 2 - q) * (n * 8)

        def experts_of(eng, expert):
            expert(0, 0, 2)
            expert(1, 1, 2)
            with eng.Fori(1, E // 2 - 1) as pair:
                expert(pair * 2, 0, 2)
                expert(pair * 2 + 1, 1, 2)
            expert(E - 2, 0, 1)
            expert(E - 1, 1, 0)

        is_first = lambda e, n: isinstance(e, int) and e < n

        @block.sync
        def _(sp):
            sp.dma_start(e_["table"][:, :], a["slots"].rearrange("(r s) w -> r (s w)", s=P)).then_inc(table_loaded, 16)

            def load(e, q):
                for name, of in WEIGHTS:
                    sp.dma_start(e_["raw_" + name][q][:, :, :], a[of].rearrange("e (k p) n -> e p k n", p=P)[e]).then_inc(w_loaded[q], 16)

            load(0, 0)
            load(1, 1)

            def expert(e, q, more):
                if more == 2:
                    sp.wait_ge(w_ready, (e + 1) * 3)
                    settle(sp)
                    load(e + 2, q)

            experts_of(sp, expert)

        @block.gpsimd
        def _(pool):
            pool.wait_ge(table_ready, 2)

            def gather(e, q):
                pool.tensor_copy(e_["gidx"][q][:, :], e_["tok"][:, bass.ds(e * CS, CS)]).then_inc(gidx_ready, 1)
                pool.wait_ge(gidx_ready, e + 1)
                settle(pool)
                for ch in range(CS):
                    r = rows(ch)
                    pool.indirect_dma_start(
                        out=e_["xg"][q][0:r, ch, :], out_offset=None, in_=a["x2n"],
                        in_offset=bass.IndirectOffsetOnAxis(ap=e_["gidx"][q][0:r, ch:ch + 1], axis=0)).then_inc(gathered[q], 16)

            gather(0, 0)
            gather(1, 1)

            def expert(e, q, more):
                if more == 2:
                    pool.wait_ge(xT_done, (e + 1) * CS)
                    settle(pool)
                    gather(e + 2, q)
                pool.tensor_copy(e_["sidx"][q][:, :], e_["tok"][:, bass.ds(e * CS, CS)]).then_inc(sidx_ready, 1)
                pool.wait_ge(sidx_ready, e + 1)
                settle(pool)
                pool.wait_ge(y_ready, (e + 1) * CS)
                settle(pool)
                if not is_first(e, 1):
                    pool.wait_ge(y_added, e * CS * 16)
                    settle(pool)
                for ch in range(CS):
                    r = rows(ch)
                    pool.indirect_dma_start(
                        out=a["out"], out_offset=bass.IndirectOffsetOnAxis(ap=e_["sidx"][q][0:r, ch:ch + 1], axis=0),
                        in_=e_["y"][q][0:r, ch, :], in_offset=None, compute_op=ALU.add).then_inc(y_added, 16)

            experts_of(pool, expert)
            pool.wait_ge(y_added, E * CS * 16)

        @block.tensor
        def _(pe):
            pe.wait_ge(table_split, 2)
            nr = E * CS
            for w in range(2):
                pe.transpose(ps["scores"][w][:, 0:nr], e_["split"][:, w, :], e_["ident"][0:nr, 0:nr]).then_inc(table_T, 1)

            def transposes(e, q, chunks):
                pe.wait_ge(gathered[q], arrived(e, q, CS))
                for ch in chunks:
                    r, m = rows(ch), e * CS + ch
                    if not (isinstance(e, int) and m < 2):
                        pe.wait_ge(xT_copied, m - 1)
                    settle(pe)
                    bank = [ps["dense"][2], ps["o"]][(q * CS + ch) % 2]
                    for k in range(DK):
                        last = pe.transpose(bank[:, k * P:k * P + r], e_["xg"][q][0:r, ch, k * P:(k + 1) * P], e_["ident"][0:r, 0:r])
                    last.then_inc(xT_done, 1)

            transposes(0, 0, range(CS))

            def expert(e, q, more):
                pe.wait_ge(w_ready, (e + 1) * 3)
                pe.wait_ge(xT_copied, (e + 1) * CS)
                if not is_first(e, 1):
                    pe.wait_ge(glu_ready, e * 2 * JB)
                for j in range(JB):
                    for n, w in enumerate(("wg", "wu")):
                        for k in range(DK):
                            last = product(pe, ps["scores"][2 * j + n][:, 0:CAP], both(e_[w][q], ALL, k, slice(j * P, (j + 1) * P)),
                                           both(e_["xT"], ALL, k, ALL), k == 0, k == DK - 1)
                        last.then_inc(gu_done, 1)
                if more:
                    transposes(e + 1, 1 - q, range(CS - 1))
                for ch in range(CS):
                    if ch == CS - 1 and more:
                        transposes(e + 1, 1 - q, [ch])
                    r, m = rows(ch), e * CS + ch
                    if not (isinstance(e, int) and m < 2):
                        pe.wait_ge(y_ready, m - 1)
                    for j in range(JB):
                        if ch == 0:
                            pe.wait_ge(h_ready, e * JB + j + 1)
                        last = product(pe, ps["dense"][(q * CS + ch) % 2][0:r, :], both(e_["hT"], ALL, j, slice(ch * P, ch * P + r)),
                                       both(e_["wd"][q], ALL, j, ALL), j == 0, j == JB - 1)
                    last.then_inc(y_done, 1)

            experts_of(pe, expert)

        @block.scalar
        def _(act):
            def weights_hi(e, q):
                act.wait_ge(w_loaded[q], arrived(e, q, 3))
                if not is_first(e, 2):
                    act.wait_ge(y_done, (e - 1) * CS)
                for name, _ in WEIGHTS:
                    act.activation(e_[name][q][0][:, :, :], e_["raw_" + name][q][:, :, :], ACT.Copy, scale=WS).then_inc(w_hi, 1)

            def copies(e, q, chunks):
                for ch in chunks:
                    r, m = rows(ch), e * CS + ch
                    act.wait_ge(xT_done, m + 1)
                    bank = [ps["dense"][2], ps["o"]][(q * CS + ch) % 2]
                    act.activation(e_["xT"][0][:, :, ch * P:ch * P + r], bank[:, :].rearrange("p (k t) -> p k t", k=DK)[:, :, 0:r],
                                   ACT.Copy, scale=XS).then_inc(xT_hi, 1)

            weights_hi(0, 0)
            copies(0, 0, range(CS))
            weights_hi(1, 1)

            def expert(e, q, more):
                for j in range(JB):
                    act.wait_ge(gu_done, e * 2 * JB + 2 * j + 1)
                    act.activation(e_["glu"][:, j, :], ps["scores"][2 * j][:, 0:CAP], ACT.Tanh, scale=0.5 / (XS * WS)).then_inc(tanh_ready, 1)
                for j in range(JB):
                    act.wait_ge(glu_ready, e * 2 * JB + 2 * j + 2)
                    act.activation(e_["hT"][0][:, j, :], e_["glu"][:, j, :], ACT.Copy, scale=HS / (XS * WS) ** 2).then_inc(h_hi, 1)
                if more:
                    copies(e + 1, 1 - q, range(CS - 1))
                if not is_first(e, 2):
                    act.wait_ge(y_added, (e - 1) * CS * 16)
                act.wait_ge(wcol_ready, e + 1)
                for ch in range(CS):
                    if ch == CS - 1 and more:
                        copies(e + 1, 1 - q, [ch])
                    r, m = rows(ch), e * CS + ch
                    act.wait_ge(y_done, m + 1)
                    act.activation(e_["y"][q][0:r, ch, :], ps["dense"][(q * CS + ch) % 2][0:r, :], ACT.Copy,
                                   scale=e_["wcol"][q][0:r, ch:ch + 1]).then_inc(y_ready, 1)
                if more == 2:
                    weights_hi(e + 2, q)

            experts_of(act, expert)

        @block.vector
        def _(dve):
            dve.wait_ge(table_loaded, 16)
            pairs_v = e_["table"][:, :].rearrange("r (s w) -> r s w", w=2)
            for w in range(2):
                dve.tensor_copy(e_["split"][:, w, :], pairs_v[:, :, w]).then_inc(table_split, 1)
            dve.wait_ge(table_T, 2)
            dve.tensor_copy(e_["tok"][:, :], ps["scores"][0][:, 0:E * CS]).then_inc(table_ready, 1)
            dve.tensor_copy(e_["w"][:, :], ps["scores"][1][:, 0:E * CS]).then_inc(table_ready, 1)
            dve.wait_ge(table_ready, 2)

            def weights_lo(e, q):
                for n, (name, _) in enumerate(WEIGHTS):
                    dve.wait_ge(w_hi, e * 3 + n + 1)
                    dve.scalar_tensor_tensor(e_[name][q][1][:, :, :], e_["raw_" + name][q][:, :, :], WS, e_[name][q][0][:, :, :],
                                             ALU.mult, ALU.subtract).then_inc(w_ready, 1)

            def copies(e, q):
                for ch in range(CS):
                    r, m = rows(ch), e * CS + ch
                    dve.wait_ge(xT_hi, m + 1)
                    bank, cols = [ps["dense"][2], ps["o"]][(q * CS + ch) % 2], slice(ch * P, ch * P + r)
                    dve.scalar_tensor_tensor(e_["xT"][1][:, :, cols], bank[:, :].rearrange("p (k t) -> p k t", k=DK)[:, :, 0:r], XS,
                                             e_["xT"][0][:, :, cols], ALU.mult, ALU.subtract).then_inc(xT_copied, 1)

            weights_lo(0, 0)
            copies(0, 0)
            weights_lo(1, 1)

            def expert(e, q, more):
                dve.tensor_copy(e_["wcol"][q][:, :], e_["w"][:, bass.ds(e * CS, CS)]).then_inc(wcol_ready, 1)
                for j in range(JB):
                    glu = e_["glu"][:, j, :]
                    dve.wait_ge(tanh_ready, e * JB + j + 1)
                    dve.scalar_tensor_tensor(glu, glu, 1.0, ps["scores"][2 * j][:, 0:CAP], ALU.add, ALU.mult).then_inc(glu_ready, 1)
                    dve.wait_ge(gu_done, e * 2 * JB + 2 * j + 2)
                    dve.wait_ge(glu_ready, e * 2 * JB + 2 * j + 1)
                    dve.tensor_tensor(glu, glu, ps["scores"][2 * j + 1][:, 0:CAP], ALU.mult).then_inc(glu_ready, 1)
                for j in range(JB):
                    dve.wait_ge(h_hi, e * JB + j + 1)
                    dve.scalar_tensor_tensor(e_["hT"][1][:, j, :], e_["glu"][:, j, :], HS / (XS * WS) ** 2, e_["hT"][0][:, j, :],
                                             ALU.mult, ALU.subtract).then_inc(h_ready, 1)
                if more:
                    copies(e + 1, 1 - q)
                if more == 2:
                    weights_lo(e + 2, q)

            experts_of(dve, expert)


LINKS = 102


def transformer_block(nc, a):
    with ExitStack() as ctx:
        def pb(name):
            return ctx.enter_context(nc.psum_tensor(name, [P, 512], F32))

        ps = {"scores": [pb(f"scores{g}") for g in range(GH)], "o": pb("o_ps"),
              "dense": [pb(f"dense{n}") for n in range(DENSE)]}
        ident = ctx.enter_context(nc.sbuf_tensor("ident", [P, P], F32))
        with ExitStack() as first:
            def sb(name, shape, dt=F32):
                return first.enter_context(nc.sbuf_tensor(name, shape, dt))

            c = {"ident": ident}
            def pair(name, shape):
                return sb(name + "_hi", shape, F16), sb(name + "_lo", shape, F16)

            c["wqkv"] = pair("wqkv", [P, DK, 3 * D])
            c["rwT"] = pair("rwT", [P, DK, E])
            for n in ("wo", "sgT", "suT", "sdT", "xT", "aT", "hT"):
                c[n] = pair(n, [P, 4, 512])
            for n in ("q", "k"):
                c["split_" + n] = pair("split_" + n, [P, HG, SEQ])
                c["stack_" + n] = sb("stack_" + n, [P, HG, GH, SEQ], F16)
            for n in ("v0", "v1", "x2n", "xres0", "xres1", "S", "pT"):
                c[n] = sb(n, [P, 4, 512])
            c["glu"], c["att"] = sb("glu", [P, 2, 512]), sb("att", [P, P])
            c["xin"] = c["x2n"]
            for n in ("v", "xres"):
                c[n] = [c[n + "0"], c[n + "1"]]
            c["bqk"] = sb("bqk", [P, 2 * HG])
            c["bv"], c["bo"], c["maskrow"] = sb("bv", [P, D]), sb("bo", [P, D]), sb("maskrow", [P, SEQ])
            c["ebias"] = sb("ebias", [P, E])
            c["ones"], c["before"] = sb("ones", [P, P]), sb("before", [P, P])
            c["nmax"], c["den"] = sb("nmax", [P, GH]), sb("den", [P, GH])
            c["rden"], c["rdenT"] = sb("rden", [P, GH, HD]), sb("rdenT", [P, P])
            c["half"] = sb("half", [P, 1])
            c["stats1"], c["stats2"] = sb("stats1", [P, TT, 6]), sb("stats2", [P, TT, 6])
            c["mv1"], c["mv2"] = sb("mv1", [P, TT, 2]), sb("mv2", [P, TT, 2])
            for n in ("sig", "sc", "sel", "wgt", "carry4", "eoff"):
                c[n] = sb(n, [P, TT, E])
            c["hi"], c["lo"] = sb("hi", [P, TT * NG, 2]), sb("lo", [P, TT * NG, 2])
            c["m1"], c["m2"] = sb("m1", [P, TT * NG]), sb("m2", [P, TT * NG])
            c["gval"], c["gout"] = sb("gval", [P, TT, NG + 8 - TOPG]), sb("gout", [P, TT, NG + 8 - TOPG])
            c["mval"], c["eout"] = sb("mval", [P, TT, E + 8 - TOPK]), sb("eout", [P, TT, E + 8 - TOPK])
            c["grep"], c["erep"], c["top8"] = sb("grep", [P, TT, 8]), sb("erep", [P, TT, 8]), sb("top8", [P, TT, 8])
            c["gmask"] = sb("gmask", [P, TT, NG])
            c["carry"], c["count"], c["wsum"] = sb("carry", [P, E]), sb("count", [P, E]), sb("wsum", [P, TT])
            c["eq"] = sb("eq", [P, TT, TOPK, E])
            c["rec"] = sb("rec", [P, TT, TOPK, 2])
            c["none"], c["idxf"], c["idx"] = sb("none", [P, TT, TOPK]), sb("idxf", [P, TT, TOPK]), sb("idx", [P, TT, TOPK], I32)
            c["tok"], c["tok_i"] = sb("tok", [P, TT]), sb("tok_i", [P, TT], I32)
            c["eoff_i"] = c["wgt"][:, :, :].bitcast(I32)
            c["fill_i"] = c["S"][0:E, 3, 0:CAPP].bitcast(I32).rearrange("e (c p) -> e c p", p=P)
            setup(nc, a, c, ps)
            sequences(nc, a, c, ps)
        with ExitStack() as second:
            def sb2(name, shape, dt=F32):
                return second.enter_context(nc.sbuf_tensor(name, shape, dt))

            nr = E * CS
            e_ = {"ident": ident, "table": sb2("table", [nr, 2 * P]), "split": sb2("split", [nr, 2, P]),
                  "tok": sb2("slot_tok", [P, nr], I32), "w": sb2("slot_w", [P, nr]),
                  "xT": [sb2(f"ex_xT_{h}", [P, DK, CAP], F16) for h in ("hi", "lo")],
                  "hT": [sb2(f"ex_hT_{h}", [P, JB, CAP], F16) for h in ("hi", "lo")],
                  "glu": sb2("ex_glu", [P, JB, CAP])}
            for n, shape in (("wg", [P, DK, IE]), ("wu", [P, DK, IE]), ("wd", [P, JB, D])):
                e_["raw_" + n] = [sb2(f"ex_raw_{n}{q}", shape) for q in range(2)]
                e_[n] = [[sb2(f"ex_{n}{q}_{h}", shape, F16) for h in ("hi", "lo")] for q in range(2)]
            for n, shape, dt in (("xg", [P, CS, D], F32), ("y", [P, CS, D], F32), ("gidx", [P, CS], I32),
                                 ("sidx", [P, CS], I32), ("wcol", [P, CS], F32)):
                e_[n] = [sb2(f"ex_{n}{q}", shape, dt) for q in range(2)]
            experts(nc, a, e_, ps)


_INS = {"x": "L0_attn_x", "Wqkv": "L0_attn_Wqkv", "bqkv": "L0_attn_bqkv", "Wo": "L0_attn_Wo", "bo": "L0_attn_bo",
        "router_w": "L0_ffn_router_w", "e_bias": "L0_ffn_e_bias", "W_gate": "L0_ffn_W_gate", "W_up": "L0_ffn_W_up",
        "W_down": "L0_ffn_W_down", "shared_gate": "L0_ffn_shared_gate", "shared_up": "L0_ffn_shared_up",
        "shared_down": "L0_ffn_shared_down"}


def kernel(**inputs):
    import concourse.bacc as _bacc
    from concourse.bass_utils import run_bass_kernel_spmd as _run

    nc = _bacc.Bacc("TRN2", target_bir_lowering=False, num_devices=1)
    arrays, a = {}, {}
    for short, name in _INS.items():
        arrays[f"in_{short}"] = np.ascontiguousarray(inputs[name])
        a[short] = nc.dram_tensor(f"in_{short}", arrays[f"in_{short}"].shape, F32, kind="ExternalInput").ap()
    a["out"] = nc.dram_tensor("out_0", (TOKENS + CAPP, D), F32, kind="ExternalOutput").ap()
    a["x2n"] = nc.dram_tensor("x2n_dram", (TOKENS + CAPP, D), F32, kind="Internal").ap()
    a["slots"] = nc.dram_tensor("slots_dram", (SLOTS, 2), F32, kind="Internal").ap()
    transformer_block(nc, a)
    r = _run(nc, [arrays], core_ids=[0])
    return np.asarray(r.results[0]["out_0"])[:TOKENS].reshape(BATCH, SEQ, D)
```
